# Optimizing a Trainium2 kernel written in Bass

```python
import numpy as np
import jax
import jax.numpy as jnp

def _softmax(x, axis=-1):
    return jax.nn.softmax(x, axis=axis)

def _gelu(x):
    return jax.nn.gelu(x, approximate=True)

def _silu(x):
    return jax.nn.silu(x)

def _sigmoid(x):
    return jax.nn.sigmoid(x)

def _layernorm(x, axis=-1, eps=1e-05):
    m = jnp.mean(x, axis=axis, keepdims=True)
    v = jnp.var(x, axis=axis, keepdims=True)
    return (x - m) / jnp.sqrt(v + eps)

def _scatter_add(tgt, idx, src, axis=0):
    return tgt.at[idx].add(src)

def _segment_sum(src, seg, n):
    return jax.ops.segment_sum(src, seg, n)
kernel_name = 'mk_conv_attn_hybrid_d2_conv_nchw512_r2_e72106'

def setup_inputs(seed: int=0):
    np.random.seed(seed)
    _w = jnp.asarray

    def _rec_inputs():
        import jax
        import jax.numpy as jnp
        _gk = jax.random.key(seed)
        x = 7.22e-05 + 1 * jax.random.normal(jax.random.fold_in(_gk, 1), (4, 256, 32, 32), jnp.float32)
        return x
    x = _rec_inputs()

    def _L0_conv_setup():
        import jax, jax.numpy as jnp
        import numpy as np
        B, C, H, W = (4, 256, 32, 32)
        C8 = C // 8
        key = jax.random.key(seed)
        ks = jax.random.split(key, 8)
        s = 0.02
        return {'x': jax.random.normal(ks[0], (B, C, H, W), dtype=jnp.float32), 'wq': jax.random.normal(ks[1], (C8, C), dtype=jnp.float32) * s, 'bq': jax.random.normal(ks[2], (C8,), dtype=jnp.float32) * s, 'wk': jax.random.normal(ks[3], (C8, C), dtype=jnp.float32) * s, 'bk': jax.random.normal(ks[4], (C8,), dtype=jnp.float32) * s, 'wv': jax.random.normal(ks[5], (C, C), dtype=jnp.float32) * s, 'bv': jax.random.normal(ks[6], (C,), dtype=jnp.float32) * s, 'gamma': jax.random.normal(ks[7], (1,), dtype=jnp.float32)}
    _L0_conv_all = _L0_conv_setup()
    _L0_conv_in = {k: v for k, v in _L0_conv_all.items() if k in ('wq', 'bq', 'wk', 'bk', 'wv', 'bv', 'gamma')}
    del _L0_conv_all

    def _L1_attn_setup():
        import jax, jax.numpy as jnp
        import numpy as np
        B, N, D_IN, D_OUT = (8, 1024, 256, 256)
        MEM_SIZE = 32

        def make_memory(num_steps, memory_size_internal):
            i = jnp.arange(num_steps)[:, None]
            j = jnp.arange(num_steps)[None, :]
            diff = i - j
            band = (diff > 0) & (diff <= memory_size_internal - 1)
            return jnp.where(band, diff, 0).astype(jnp.float32)
        key = jax.random.key(seed)
        k1, k2, k3, k4 = jax.random.split(key, 4)
        limit = float(np.sqrt(6.0 / (D_IN + D_OUT)))
        return {'input_data': jax.random.normal(k1, (B, N, D_IN), dtype=jnp.float32), 'W1': jax.random.uniform(k2, (D_IN, D_OUT), minval=-limit, maxval=limit, dtype=jnp.float32), 'W2': jax.random.uniform(k3, (D_IN, D_OUT), minval=-limit, maxval=limit, dtype=jnp.float32), 'bias': jax.random.normal(k4, (D_OUT,), dtype=jnp.float32)}
    _L1_attn_all = _L1_attn_setup()
    _L1_attn_in = {k: v for k, v in _L1_attn_all.items() if k in ('W1', 'W2', 'bias')}
    del _L1_attn_all

    def _L1_ffn_setup():
        import jax, jax.numpy as jnp
        import numpy as np
        TOP_K = 2
        key = jax.random.key(seed)
        k1, k2, k3, k4 = jax.random.split(key, 4)
        B, S, d = (4, 1024, 256)
        E, H = (32, 64)
        x = jax.random.normal(k1, (B, S, d), dtype=jnp.float32)
        expert_sel = jax.random.normal(k2, (E, d), dtype=jnp.float32) / np.sqrt(d).astype(np.float32)
        keys = jax.random.normal(k3, (E, d, H), dtype=jnp.float32) / np.sqrt(d).astype(np.float32)
        values = jax.random.normal(k4, (E, H, d), dtype=jnp.float32) / np.sqrt(E * H).astype(np.float32)
        return {'x': x, 'expert_sel': expert_sel, 'keys': keys, 'values': values}
    _L1_ffn_all = _L1_ffn_setup()
    _L1_ffn_in = {k: v for k, v in _L1_ffn_all.items() if k in ('expert_sel', 'keys', 'values')}
    del _L1_ffn_all
    return {'x': x, 'L0_conv_wq': _L0_conv_in['wq'], 'L0_conv_bq': _L0_conv_in['bq'], 'L0_conv_wk': _L0_conv_in['wk'], 'L0_conv_bk': _L0_conv_in['bk'], 'L0_conv_wv': _L0_conv_in['wv'], 'L0_conv_bv': _L0_conv_in['bv'], 'L0_conv_gamma': _L0_conv_in['gamma'], 'L1_attn_W1': _L1_attn_in['W1'], 'L1_attn_W2': _L1_attn_in['W2'], 'L1_attn_bias': _L1_attn_in['bias'], 'L1_ffn_expert_sel': _L1_ffn_in['expert_sel'], 'L1_ffn_keys': _L1_ffn_in['keys'], 'L1_ffn_values': _L1_ffn_in['values']}

def reference(x, L0_conv_wq, L0_conv_bq, L0_conv_wk, L0_conv_bk, L0_conv_wv, L0_conv_bv, L0_conv_gamma, L1_attn_W1, L1_attn_W2, L1_attn_bias, L1_ffn_expert_sel, L1_ffn_keys, L1_ffn_values):
    import jax
    import jax.numpy as jnp

    def _L0_conv_ref(x, wq, bq, wk, bk, wv, bv, gamma):
        import jax, jax.numpy as jnp
        import numpy as np
        B, C, H, W = (4, 256, 32, 32)
        C8 = C // 8
        b, c, h, w = x.shape
        q = jnp.einsum('bchw,oc->bohw', x, wq) + bq[None, :, None, None]
        k = jnp.einsum('bchw,oc->bohw', x, wk) + bk[None, :, None, None]
        v = jnp.einsum('bchw,oc->bohw', x, wv) + bv[None, :, None, None]
        qf = q.reshape(b, c // 8, h * w)
        kf = k.reshape(b, c // 8, h * w)
        energy = jnp.einsum('bci,bcj->bij', qf, kf).reshape(b, h, w, h, w)
        attn = jax.nn.softmax(energy, axis=-1)
        out = jnp.einsum('bchk,bhwkv->bcwv', v, attn)
        return gamma * out + x

    def _L1_attn_ref(input_data, W1, W2, bias):
        import jax, jax.numpy as jnp
        import numpy as np
        B, N, D_IN, D_OUT = (8, 1024, 256, 256)
        MEM_SIZE = 32

        def make_memory(num_steps, memory_size_internal):
            i = jnp.arange(num_steps)[:, None]
            j = jnp.arange(num_steps)[None, :]
            diff = i - j
            band = (diff > 0) & (diff <= memory_size_internal - 1)
            return jnp.where(band, diff, 0).astype(jnp.float32)
        num_steps = input_data.shape[1]
        memory = make_memory(num_steps, MEM_SIZE + 1)
        h_hatt = jnp.einsum('nm,bmd->bnd', memory, input_data)
        h = jnp.einsum('bnd,de->bne', input_data, W1)
        h = h + jnp.einsum('bnd,de->bne', h_hatt, W2) + bias
        return h

    def _L1_ffn_ref(x, expert_sel, keys, values):
        import jax, jax.numpy as jnp
        import numpy as np
        TOP_K = 2
        B, S, d = x.shape
        E = keys.shape[0]
        xt = x.reshape(-1, d)
        T = xt.shape[0]
        sel = jax.nn.sigmoid(xt @ expert_sel.T)
        sel_val, sel_idx = jax.lax.top_k(sel, TOP_K)
        w = jnp.zeros((T, E), dtype=xt.dtype).at[jnp.arange(T)[:, None], sel_idx].add(sel_val)
        h = jax.nn.relu(jnp.einsum('td,edh->teh', xt, keys))
        out = jnp.einsum('teh,te,ehv->tv', h, w, values)
        return out.reshape(B, S, -1)

    def _gn(v, G=32, eps=1e-05):
        B_, C_, H_, W_ = v.shape
        g = v.reshape(B_, G, C_ // G, H_, W_)
        m = jnp.mean(g, axis=(2, 3, 4), keepdims=True)
        s = jnp.var(g, axis=(2, 3, 4), keepdims=True)
        return ((g - m) / jnp.sqrt(s + eps)).reshape(v.shape)

    def _ln_c(v, eps=1e-06):
        m = jnp.mean(v, axis=1, keepdims=True)
        s = jnp.var(v, axis=1, keepdims=True)
        return (v - m) / jnp.sqrt(s + eps)

    def _ln_t(v, eps=1e-05):
        m = jnp.mean(v, axis=-1, keepdims=True)
        s = jnp.var(v, axis=-1, keepdims=True)
        return (v - m) / jnp.sqrt(s + eps)

    def _to_tokens(v):
        B_, C_, H_, W_ = v.shape
        return v.reshape(B_, C_, H_ * W_).transpose(0, 2, 1)

    def _from_tokens(t, like):
        B_, C_, H_, W_ = like.shape
        return t.transpose(0, 2, 1).reshape(B_, C_, H_, W_)
    x = _L0_conv_ref(x, L0_conv_wq, L0_conv_bq, L0_conv_wk, L0_conv_bk, L0_conv_wv, L0_conv_bv, L0_conv_gamma)
    t = _to_tokens(x)
    t = t + _L1_attn_ref(_ln_t(t), L1_attn_W1, L1_attn_W2, L1_attn_bias)
    t = t + _L1_ffn_ref(_ln_t(t), L1_ffn_expert_sel, L1_ffn_keys, L1_ffn_values)
    x = _from_tokens(t, x)
    return x

_drawn_inputs = setup_inputs


def setup_inputs(seed=0):
    import zlib

    import numpy as np

    out = dict(_drawn_inputs(seed))
    spreads = {}
    factors = {'L0_conv_wq': 6.889,
     'L0_conv_bq': 8.0,
     'L0_conv_wk': 6.755,
     'L0_conv_bk': 8.0,
     'L1_attn_W1': 6.166,
     'L1_attn_bias': 6.704,
     'L1_ffn_expert_sel': 8.0,
     'L1_ffn_keys': 8.0,
     'L1_ffn_values': 8.0}
    for name, (base, spread) in spreads.items():
        noise = np.random.default_rng([zlib.crc32(name.encode()), seed]).standard_normal(out[name].shape)
        drawn = base * np.exp(spread * noise) if base else spread * noise
        out[name] = jnp.asarray(drawn.astype(out[name].dtype))
    for name, factor in factors.items():
        out[name] = (out[name] * factor).astype(out[name].dtype)
    return out
```

```python
import concourse.bass as bass
from concourse import mybir
from contextlib import ExitStack
import itertools

F32 = mybir.dt.float32
BF16 = mybir.dt.bfloat16
I32 = mybir.dt.int32
U32 = mybir.dt.uint32
ALU = mybir.AluOpType
ACT = mybir.ActivationFunctionType
AX = mybir.AxisListType

P = 128
B, C, H, W = 4, 256, 32, 32
HW = H * W
N = B * HW
TB = HW // P
NT = N // P
CH = C // P
QK = C // 8
WT = P // H
KB = W // WT
REACH = 32
NE, HID = 32, 64
CAP = N + P
ROW = C + 2
ID, WEIGHT = C, C + 1
SLOT_TILES = 2 * N // P + NE
GROUP = 4
LN_EPS = 1e-5
PADROW = 2 * N

S_AV, S_MIX, S_SEL, S_POS = 1, 2, 3, 4
LAST = S_POS


def attention_moe(nc, x_cm, x_tok, wqT, bq, wkT, bk, wvT, bv, gamma, w1, w2, bias, selT, keys, values, out):
    slots_d = nc.dram_tensor("slot_rows", [NE * CAP, ROW], F32, kind="Internal").ap()
    pair_d = nc.dram_tensor("expert_outputs", [2 * N, C], F32, kind="Internal").ap()

    with ExitStack() as ctx:
        def sb(name, shape, dt=F32):
            return ctx.enter_context(nc.sbuf_tensor(name, shape, dt))

        def ps(name, shape, dt=F32):
            return ctx.enter_context(nc.psum_tensor(name, shape, dt))

        def sem(name):
            return ctx.enter_context(nc.semaphore(name))

        wqk = sb("wqk", [P, CH, P])
        bqk = sb("bqk", [P, 1])
        wv = sb("wv", [P, CH, C])
        gbv = sb("gbv", [P, C])
        gam = sb("gam", [P, 1])
        w1s = sb("w1s", [P, CH, C])
        w2s = sb("w2s", [P, CH, C])
        biasb = sb("biasb", [P, C])
        sels = sb("sels", [P, CH, NE])
        keys_s = sb("keys_s", [P, CH, NE, HID])
        values_s = sb("values_s", [HID, NE, C])
        ident = sb("ident", [P, P])
        band = sb("band", [P, P + REACH])
        upper = sb("upper", [P, P], BF16)
        ones_b = sb("ones_b", [P, P], BF16)
        ones_f = sb("ones_f", [P, NE])
        iota_e = sb("iota_e", [P, NE])
        ebase = sb("ebase", [P, NE])
        iota_p = sb("iota_p", [P, 1])
        out_ids = sb("out_ids", [P, NT, 2], I32)
        pad_tile = sb("pad_tile", [P, ROW])
        half_neg = sb("half_neg", [P, 1])

        xc = sb("xc", [P, 2, CH, HW])
        q_s = sb("q_s", [2 * QK, 2, HW])
        k_s = sb("k_s", [2 * QK, 2, WT, KB, W])
        vT = sb("vT", [P, 2, KB, C])
        xt = sb("xt", [P, 4, C])
        prob = sb("prob", [P, 2, KB * WT, W])
        gmax = sb("gmax", [P, 2, WT * KB])
        gsum = sb("gsum", [P, 2, WT * KB])
        ginv = sb("ginv", [P, 2, WT * KB])
        t1 = sb("t1", [P, 2, C])
        t1b = sb("t1b", [P, 2, C])
        bn1 = sb("bn1", [P, 2, 6])
        mv1 = sb("mv1", [P, 2, 2])
        rstd1 = sb("rstd1", [P, 2, 2])
        u1 = sb("u1", [P, 3, C])
        uh = sb("uh", [P, 2, CH, 2, P])
        t2 = sb("t2", [P, NT, C])
        bn2 = sb("bn2", [P, 2, 6])
        mv2 = sb("mv2", [P, 2, 2])
        rstd2 = sb("rstd2", [P, 2, 2])
        rows = sb("rows", [P, 4, 2, ROW])
        u2T = sb("u2T", [P, 2, CH, P])
        ex = sb("ex", [P, 2, NE])
        ex1 = sb("ex1", [P, 2, NE])
        sig = sb("sig", [P, 2, NE])
        top = sb("top", [P, 2, 8])
        topi = sb("topi", [P, 2, 8], U32)
        topf = sb("topf", [P, 2, 2])
        hot = sb("hot", [P, 2, 2, NE])
        hotb = sb("hotb", [P, 2, NE], BF16)
        seen = sb("seen", [P, NE], BF16)
        spot = sb("spot", [P, 2, NE])
        picked = sb("picked", [P, 2, 2, NE])
        slotf = sb("slotf", [P, 2, 2])
        slot = sb("slot", [P, 4, 2], I32)

        cnt = sb("cnt", [P, NE])
        tiles_i = sb("tiles_i", [P, NE], I32)
        tiles_f = sb("tiles_f", [P, NE])
        tincl = sb("tincl", [P, NE])
        texcl = sb("texcl", [P, NE])
        at_i = sb("at_i", [P, NE])
        at_x = sb("at_x", [P, NE])
        rowt = sb("rowt", [P, NE])
        padr = sb("padr", [P, NE])
        padr_i = sb("padr_i", [1, NE], I32)
        sched = sb("sched", [P, 2])
        sums = sb("sums", [P, 2])
        i128 = sb("i128", [P, 1])
        used = sb("used", [P, 1])
        term = sb("term", [P, 2])
        junk = sb("junk", [P, 2, NE])
        sched_i = sb("sched_i", [1, 2, P], I32)

        xin = sb("xin", [P, 2, GROUP, ROW])
        dest = sb("dest", [P, 2, GROUP], I32)
        wgt = sb("wgt", [P, 2, GROUP])
        uT = sb("uT", [P, GROUP, CH, P])
        hid = sb("hid", [P, GROUP, P])
        hT = sb("hT", [HID, GROUP, P])
        yb = sb("yb", [P, 2, GROUP, C])

        E = ps("E", [P, WT * KB * W])
        bank = {i: ps(f"bank{i}", [P, 512]) for i in range(2, 8)}
        av_p = bank[2][:, 0:C]
        mix_p = bank[3][:, :].rearrange("p (a s n) -> p a s n", a=CH, s=2)
        h_p = bank[4][:, 0:C]
        t2_p = bank[5][:, 0:C].rearrange("p (a n) -> p a n", a=CH)
        lg_p = bank[6][:, 0:NE]
        pos_p = bank[6][:, NE:2 * NE]
        bank7 = bank[7]
        cnt_p = bank[6][:, 0:NE]
        sched_p = bank[2][0:1, 0:2 * P]
        T_p = [E[:, q * 512:(q + 1) * 512].rearrange("p (k a n) -> p k a n", k=2, a=CH) for q in range(2)]
        H_p = [bank[2 + q][:, 0:2 * HID].rearrange("p (k n) -> p k n", k=2) for q in range(2)]
        HT_p = [bank[4 + q][:, 0:2 * P].rearrange("p (k n) -> p k n", k=2) for q in range(2)]
        Y_p = [bank[6 + q][:, :].rearrange("p (k n) -> p k n", k=2) for q in range(2)]

        ld_wproj, ld_wmix, ld_bcast, ld_keys = sem("ld_wproj"), sem("ld_wmix"), sem("ld_bcast"), sem("ld_keys")
        ld_xc = [sem(f"ld_xc{i}") for i in range(2)]
        ld_xt = [sem(f"ld_xt{i}") for i in range(4)]
        const_raw, const_done, gbv_done = sem("const_raw"), sem("const_done"), sem("gbv_done")
        qk_mm, q_out, k_out, v_mm, v_out = sem("qk_mm"), sem("q_out"), sem("k_out"), sem("v_mm"), sem("v_out")
        e_mm, max_done, centred, exp_done = sem("e_mm"), sem("max_done"), sem("centred"), sem("exp_done")
        sum_done, inv_done, prob_done, av_mm = sem("sum_done"), sem("inv_done"), sem("prob_done"), sem("av_mm")
        t1_done, bn1_done, mv1_done, ve1_done = sem("t1_done"), sem("bn1_done"), sem("mv1_done"), sem("ve1_done")
        rstd1_done, u1_done, t1b_done = sem("rstd1_done"), sem("u1_done"), sem("t1b_done")
        mix_mm, uh_out, h_mm, t2_done = sem("mix_mm"), sem("uh_out"), sem("h_mm"), sem("t2_done")
        bn2_done, mv2_done, ve2_done, rstd2_done = sem("bn2_done"), sem("mv2_done"), sem("ve2_done"), sem("rstd2_done")
        u2_done, u2_copied, u2T_mm, u2T_out = sem("u2_done"), sem("u2_copied"), sem("u2T_mm"), sem("u2T_out")
        lg_mm, ex_done, ex1_done, sig_done = sem("lg_mm"), sem("ex_done"), sem("ex1_done"), sem("sig_done")
        top_done, topi_done, topf_done, hot_done = sem("top_done"), sem("topi_done"), sem("topf_done"), sem("hot_done")
        hotb_done, pos_mm, seen_done, spot_done = sem("hotb_done"), sem("pos_mm"), sem("seen_done"), sem("spot_done")
        slotf_done, slot_done, cols_done = sem("slotf_done"), sem("slot_done"), sem("cols_done")
        scattered = [sem(f"scattered{i}") for i in range(4)]
        cnt_mm, plan, padr_done, term_done = sem("cnt_mm"), sem("plan"), sem("padr_done"), sem("term_done")
        sched_done, sched_mm, sched_out, pads_filled = sem("sched_done"), sem("sched_mm"), sem("sched_out"), sem("pads_filled")
        ld_rows = [sem(f"ld_rows{i}") for i in range(2)]
        cols_out, T_mm, T_out, H_mm, hid_out = sem("cols_out"), sem("T_mm"), sem("T_out"), sem("H_mm"), sem("hid_out")
        HT_mm, HT_out, Y_mm, y_out_a, y_out_v = sem("HT_mm"), sem("HT_out"), sem("Y_mm"), sem("y_out_a"), sem("y_out_v")
        y_sent = [sem(f"y_sent{i}") for i in range(2)]
        ld_pair = [sem(f"ld_pair{i}") for i in range(2)]
        half_sum, out_sum = sem("half_sum"), sem("out_sum")
        stored = [sem(f"stored{i}") for i in range(2)]

        def after(eng, s, n):
            if not isinstance(n, int) or n > 0:
                eng.wait_ge(s, n)

        def computed(eng, value):
            if isinstance(value, int):
                return value
            reg = eng.alloc_register(f"wait_value_{next(number)}")
            eng.reg_mov(reg, value)
            return eng.snap(reg)

        number = itertools.count()
        ITER = SLOT_TILES // (2 * GROUP)
        CG = 4
        NC_ = NT // CG
        fin = prob[:, :, :, :].rearrange("p a b c -> p a (b c)").rearrange("p a (t n) -> p a t n", n=C)
        pair0 = yb
        pair1 = xc[:, 0, :, :].rearrange("p a n -> p (a n)").rearrange("p (a t n) -> p a t n", a=2, n=C)

        def proj_work(s):
            b, j = s // TB + 1, s % TB
            if b >= B:
                return None
            return b, j, ([j - (TB - 2)] if j >= TB - 2 else [])

        def v_no(b, j):
            return b * KB + j

        block = ctx.enter_context(nc.Block())

        @block.sync
        def _(sp):
            half = "(a p) n -> p a n"
            sp.dma_start(xc[:, 0, :, :], x_cm[:, 0:HW].rearrange(half, p=P)).then_inc(ld_xc[0], 16)
            for r in range(2):
                sp.dma_start(wqk[:, :, r * QK:(r + 1) * QK], wqT.rearrange(half, p=P)).then_inc(ld_wproj, 16)
                sp.dma_start(wqk[:, :, (2 + r) * QK:(3 + r) * QK], wkT.rearrange(half, p=P)).then_inc(ld_wproj, 16)
                sp.dma_start(bqk[r * QK:(r + 1) * QK, :], bq).then_inc(ld_wproj, 16)
                sp.dma_start(bqk[(2 + r) * QK:(3 + r) * QK, :], bk).then_inc(ld_wproj, 16)
            sp.dma_start(wv[:, :, :], wvT.rearrange(half, p=P)).then_inc(ld_wproj, 16)
            sp.dma_start(gbv[:, :], bv.to_broadcast([P, C])).then_inc(ld_bcast, 16)
            sp.dma_start(gam[:, :], gamma.to_broadcast([P, 1])).then_inc(ld_bcast, 16)
            sp.dma_start(biasb[:, :], bias.to_broadcast([P, C])).then_inc(ld_bcast, 16)
            sp.dma_start(xc[:, 1, :, :], x_cm[:, HW:2 * HW].rearrange(half, p=P)).then_inc(ld_xc[1], 16)
            sp.dma_start(w1s[:, :, :], w1.rearrange(half, p=P)).then_inc(ld_wmix, 16)
            sp.dma_start(w2s[:, :, :], w2.rearrange(half, p=P)).then_inc(ld_wmix, 16)
            sp.dma_start(sels[:, :, :], selT.rearrange(half, p=P)).then_inc(ld_wmix, 16)
            for t in range(NT):
                if t == 4:
                    sp.dma_start(keys_s[:, :, :, :], keys.rearrange("(a p) e h -> p a e h", p=P)).then_inc(ld_keys, 16)
                    sp.dma_start(values_s[:, :, :], values).then_inc(ld_keys, 16)
                if t >= 4:
                    sp.wait_ge(t1_done, t - 3)
                sp.dma_start(xt[:, t % 4, :], x_tok[t * P:(t + 1) * P, :]).then_inc(ld_xt[t % 4], 16)
                b = t // TB + 2
                if t % TB == 4 and 2 <= b < B:
                    sp.wait_ge(v_mm, v_no(b - 2, KB - 1) + 1)
                    sp.wait_ge(qk_mm, 2 * (b - 1))
                    sp.dma_start(xc[:, b % 2, :, :],
                                 x_cm[:, b * HW:(b + 1) * HW].rearrange(half, p=P)).then_inc(ld_xc[b % 2], 16)

            sp.wait_ge(const_done, 1)
            sp.wait_ge(padr_done, 1)
            with sp.Fori(0, NE) as e:
                first = sp.value_load(padr_i[0:1, bass.ds(e, 1)], min_val=0, max_val=NE * CAP - P)
                sp.dma_start(slots_d[bass.ds(first, P), :], pad_tile[:, :]).then_inc(pads_filled, 16)
            sp.wait_ge(pads_filled, 16 * NE)
            for i in range(4):
                sp.wait_ge(scattered[i], 2 * 16 * (NT // 4))
            sp.wait_ge(sched_out, 1)
            def round_(i):
                for g in range(2):
                    first = [sp.value_load(sched_i[0:1, 1, bass.ds(i * (2 * GROUP) + (g * GROUP + k), 1)],
                                           min_val=0, max_val=NE * CAP - P) for k in range(GROUP)]
                    transposed = computed(sp, i * 4 + 2 * g)
                    copied = computed(sp, i * 4 + 2 * g)
                    sp.wait_ge(sched_out, 1)
                    after(sp, T_mm, transposed)
                    after(sp, cols_out, copied)
                    for k in range(GROUP):
                        sp.dma_start(xin[:, g, k, :], slots_d[bass.ds(first[k], P), :]).then_inc(ld_rows[g], 16)

            round_(0)
            with sp.Fori(1, ITER) as i:
                round_(i)

            for g in range(2):
                sp.wait_ge(y_sent[g], 16 * SLOT_TILES // 2)
            for c in range(NC_):
                if c >= 2:
                    sp.wait_ge(out_sum, c - 1)
                for r, buf in enumerate((pair0, pair1)):
                    src = pair_d[r * N + c * CG * P:r * N + (c + 1) * CG * P, :]
                    sp.dma_start(buf[:, c % 2, :, :], src.rearrange("(t p) n -> p t n", p=P)).then_inc(ld_pair[c % 2], 16)

        @block.gpsimd
        def _(pool):
            g = nc.gpsimd
            g.memset(ident[:, :], 0.0).then_inc(const_raw, 1)
            g.memset(upper[:, :], 1.0).then_inc(const_raw, 1)
            g.iota(band[:, :], pattern=[[1, P + REACH]], base=0, channel_multiplier=-1,
                   allow_small_or_imprecise_dtypes=True).then_inc(const_raw, 1)
            g.memset(pad_tile[:, :], 0.0).then_inc(const_raw, 1)
            g.memset(half_neg[:, :], -0.5)
            g.memset(ones_b[:, :], 1.0)
            g.memset(ones_f[:, :], 1.0)
            g.memset(seen[:, :], 0.0)
            g.memset(hid[:, :, :], 0.0)
            g.iota(iota_e[:, :], pattern=[[1, NE]], base=0, channel_multiplier=0, allow_small_or_imprecise_dtypes=True)
            g.iota(ebase[:, :], pattern=[[CAP, NE]], base=0, channel_multiplier=0, allow_small_or_imprecise_dtypes=True)
            g.iota(iota_p[:, :], pattern=[[0, 1]], base=0, channel_multiplier=1, allow_small_or_imprecise_dtypes=True)
            g.iota(i128[:, :], pattern=[[0, 1]], base=0, channel_multiplier=P, allow_small_or_imprecise_dtypes=True)
            g.iota(out_ids[:, :, :], pattern=[[P, NT], [N, 2]], base=0, channel_multiplier=1).then_inc(const_raw, 1)
            pool.wait_ge(const_raw, 5)
            g.affine_select(out=ident[:, :], in_=ident[:, :], compare_op=ALU.not_equal, fill=1.0, base=0,
                            pattern=[[-1, P]], channel_multiplier=1).then_inc(const_raw, 1)
            g.affine_select(out=upper[:, :], in_=upper[:, :], compare_op=ALU.is_gt, fill=0.0, base=0,
                            pattern=[[1, P]], channel_multiplier=-1).then_inc(const_raw, 1)
            g.affine_select(out=band[:, :], in_=band[:, :], compare_op=ALU.is_gt, fill=0.0, base=0,
                            pattern=[[1, P + REACH]], channel_multiplier=-1).then_inc(const_raw, 1)
            g.iota(pad_tile[:, ID:ID + 1].bitcast(I32), pattern=[[0, 1]], base=PADROW,
                   channel_multiplier=1).then_inc(const_raw, 1)
            pool.wait_ge(const_raw, 9)
            g.affine_select(out=band[:, :], in_=band[:, :], compare_op=ALU.is_ge, fill=0.0, base=REACH,
                            pattern=[[-1, P + REACH]], channel_multiplier=1).then_inc(const_done, 1)

            for s in range(NT + LAST):
                t = s - S_POS
                if 0 <= t:
                    pool.wait_ge(slot_done, t + 1)
                    pool.wait_ge(u2_copied, t + 1)
                    after(pool, scattered[t % 4], 32 * (t // 4))
                    g.tensor_copy(rows[:, t % 4, :, ID].bitcast(I32), out_ids[:, t, :]).then_inc(cols_done, 1)
                    g.tensor_copy(rows[:, t % 4, :, WEIGHT], top[:, t % 2, 0:2]).then_inc(cols_done, 1)
                    pool.wait_ge(cols_done, 2 * t + 2)
                    for r in range(2):
                        g.indirect_dma_start(
                            out=slots_d, out_offset=bass.IndirectOffsetOnAxis(ap=slot[:, t % 4, r:r + 1], axis=0),
                            in_=rows[:, t % 4, r, :], in_offset=None).then_inc(scattered[t % 4], 16)
                t = s
                if t < NT:
                    pool.wait_ge(inv_done, t + 1)
                    g.tensor_tensor(prob[:, t % 2], prob[:, t % 2],
                                    ginv[:, t % 2].unsqueeze(2).to_broadcast([P, WT * KB, W]),
                                    ALU.mult).then_inc(prob_done, 1)
                t = s - S_AV
                if 0 <= t < NT:
                    pool.wait_ge(mv1_done, t + 1)
                    after(pool, u1_done, t - 1)
                    g.tensor_scalar(rstd1[:, t % 2, 0:1], mv1[:, t % 2, 1:2], LN_EPS, None, ALU.add).then_inc(ve1_done, 1)
                    pool.wait_ge(ve1_done, t + 1)
                    g.tensor_tensor(rstd1[:, t % 2, 1:2], rstd1[:, t % 2, 0:1], half_neg[:, :], ALU.pow).then_inc(rstd1_done, 1)
                    after(pool, t2_done, t - 1)
                    if t == 0:
                        pool.wait_ge(ld_bcast, 48)
                    g.tensor_tensor(t1b[:, t % 2], t1[:, t % 2], biasb[:, :], ALU.add).then_inc(t1b_done, 1)
                t = s - S_MIX
                if 0 <= t < NT:
                    pool.wait_ge(mv2_done, t + 1)
                    after(pool, u2_done, t - 1)
                    g.tensor_scalar(rstd2[:, t % 2, 0:1], mv2[:, t % 2, 1:2], LN_EPS, None, ALU.add).then_inc(ve2_done, 1)
                    pool.wait_ge(ve2_done, t + 1)
                    g.tensor_tensor(rstd2[:, t % 2, 1:2], rstd2[:, t % 2, 0:1], half_neg[:, :], ALU.pow).then_inc(rstd2_done, 1)

            def round_(i):
                for gr in range(2):
                    for k in range(GROUP):
                        ready = y_out_a if k < 2 else y_out_v
                        copied = computed(pool, i * 4 + 2 * gr + 1)
                        weighted = computed(pool, i * 4 + (2 * gr + k % 2 + 1))
                        pool.wait_ge(sched_out, 1)
                        pool.wait_ge(cols_out, copied)
                        pool.wait_ge(ready, weighted)
                        g.indirect_dma_start(
                            out=pair_d, out_offset=bass.IndirectOffsetOnAxis(ap=dest[:, gr, k:k + 1], axis=0),
                            in_=yb[:, gr, k, :], in_offset=None,
                            bounds_check=2 * N - 1, oob_is_err=False).then_inc(y_sent[gr], 16)

            round_(0)
            with pool.Fori(1, ITER) as i:
                round_(i)

        @block.scalar
        def _(act):
            a = nc.scalar

            def q_evac(b, c):
                act.wait_ge(qk_mm, 2 * b + c + 1)
                after(act, e_mm, TB * (b - 1))
                a.activation(q_s[:, b % 2, c * 512:(c + 1) * 512], bank7[0:2 * QK, :], ACT.Identity,
                             bias=bqk[0:2 * QK, 0:1]).then_inc(q_out, 1)

            for c in range(2):
                q_evac(0, c)
            for s in range(NT + LAST):
                t = s - S_MIX
                if 0 <= t < NT:
                    act.wait_ge(mix_mm, t + 1)
                    after(act, h_mm, t - 1)
                    a.activation(uh[:, t % 2], mix_p, ACT.Copy).then_inc(uh_out, 1)
                t = s - S_SEL
                if 0 <= t < NT:
                    act.wait_ge(u2T_mm, t + 1)
                    after(act, lg_mm, t - 1)
                    a.activation(u2T[:, t % 2], t2_p, ACT.Copy).then_inc(u2T_out, 1)
                t = s
                if t < NT:
                    act.wait_ge(centred, t + 1)
                    a.activation(prob[:, t % 2], prob[:, t % 2], ACT.Exp).then_inc(exp_done, 1)
                t = s - S_SEL
                if 0 <= t < NT:
                    act.wait_ge(lg_mm, t + 1)
                    after(act, ex1_done, t - 1)
                    a.activation(ex[:, t % 2], lg_p, ACT.Exp, scale=-1.0).then_inc(ex_done, 1)
                work = proj_work(s)
                if work:
                    for c in work[2]:
                        q_evac(work[0], c)
                t = s - S_MIX
                if 0 <= t < NT:
                    act.wait_ge(u2_done, t + 1)
                    a.activation(rows[:, t % 4, 1, 0:C], rows[:, t % 4, 0, 0:C], ACT.Copy).then_inc(u2_copied, 1)

            def round_(i):
                for g in range(2):
                    for q in range(2):
                        act.wait_ge(T_mm, i * 4 + (2 * g + q + 1))
                        after(act, H_mm, i * 4 + 2 * g)
                        a.activation(uT[:, 2 * q:2 * q + 2], T_p[q], ACT.Copy).then_inc(T_out, 1)
                    after(act, y_sent[g], i * (16 * GROUP))
                    act.wait_ge(cols_out, i * 4 + 2 * g + 2)
                    act.wait_ge(Y_mm, i * 4 + (2 * g + 1))
                    for k in range(2):
                        a.activation(yb[:, g, k, :], Y_p[0][:, k, :], ACT.Copy, scale=wgt[:, g, k:k + 1]).then_inc(y_out_a, 1)

            round_(0)
            with act.Fori(1, ITER) as i:
                round_(i)

            for c in range(NC_):
                act.wait_ge(out_sum, c + 1)
                rows_out = out[c * CG * P:(c + 1) * CG * P, :].rearrange("(t p) n -> p t n", p=P)
                act.dma_start(rows_out, fin[:, c % 2]).then_inc(stored[c % 2], 16)
            for i in range(2):
                act.wait_ge(stored[i], 16 * (NC_ // 2))

        @block.vector
        def _(dve):
            v = nc.vector

            def k_evac(b, c):
                dve.wait_ge(qk_mm, 2 * b + c + 1)
                after(dve, e_mm, TB * (b - 1))
                cols = k_s[:, b % 2, :, :, c * 16:(c + 1) * 16].rearrange("p g j v -> p v j g")
                src = bank7[2 * QK:4 * QK, :].rearrange("p (v j g) -> p v j g", v=16, g=WT)
                v.tensor_scalar(cols, src, bqk[2 * QK:4 * QK, 0:1], None, ALU.add).then_inc(k_out, 1)

            def v_evac(b, j):
                dve.wait_ge(v_mm, v_no(b, j) + 1)
                after(dve, av_mm, TB * (b - 1))
                v.scalar_tensor_tensor(out=vT[:, b % 2, j, :], in0=bank7[:, 0:C], scalar=gam[:, 0:1], in1=gbv[:, :],
                                       op0=ALU.mult, op1=ALU.add).then_inc(v_out, 1)

            dve.wait_ge(ld_bcast, 48)
            v.tensor_scalar(gbv[:, :], gbv[:, :], gam[:, 0:1], None, ALU.mult).then_inc(gbv_done, 1)
            dve.wait_ge(ld_wproj, 16 * 9)
            for c in range(2):
                k_evac(0, c)
            dve.wait_ge(gbv_done, 1)
            for j in range(KB):
                v_evac(0, j)
            dve.wait_ge(const_done, 1)

            for s in range(NT + LAST):
                t = s
                if t < NT:
                    dve.wait_ge(e_mm, t + 1)
                    e3 = E[:, :].rearrange("p (a v) -> p a v", v=W)
                    v.tensor_reduce(gmax[:, t % 2], e3, AX.X, ALU.max).then_inc(max_done, 1)
                    dve.wait_ge(max_done, t + 1)
                    after(dve, av_mm, t - 1)
                    v.tensor_tensor(prob[:, t % 2].rearrange("p (j w) v -> p w j v", w=WT),
                                    E[:, :].rearrange("p (w j v) -> p w j v", w=WT, v=W),
                                    gmax[:, t % 2].rearrange("p (w j) -> p w j", w=WT).unsqueeze(3)
                                    .to_broadcast([P, WT, KB, W]), ALU.subtract).then_inc(centred, 1)
                t = s - S_POS
                if 0 <= t:
                    dve.wait_ge(pos_mm, t + 1)
                    v.tensor_tensor(spot[:, t % 2], pos_p, ebase[:, :], ALU.add).then_inc(spot_done, 1)
                    v.tensor_tensor(seen[:, :], seen[:, :], hotb[:, t % 2], ALU.add).then_inc(seen_done, 1)
                    dve.wait_ge(spot_done, t + 1)
                    for r in range(2):
                        v.tensor_tensor_reduce(picked[:, t % 2, r], hot[:, t % 2, r], spot[:, t % 2], 1.0, 0.0,
                                               ALU.mult, ALU.add, slotf[:, t % 2, r:r + 1]).then_inc(slotf_done, 1)
                    dve.wait_ge(slotf_done, 2 * t + 2)
                    after(dve, scattered[t % 4], 32 * (t // 4))
                    v.tensor_copy(slot[:, t % 4], slotf[:, t % 2]).then_inc(slot_done, 1)
                t = s
                if t < NT:
                    dve.wait_ge(exp_done, t + 1)
                    v.tensor_reduce(gsum[:, t % 2], prob[:, t % 2], AX.X, ALU.add).then_inc(sum_done, 1)
                    dve.wait_ge(sum_done, t + 1)
                    after(dve, prob_done, t - 1)
                    v.reciprocal(ginv[:, t % 2], gsum[:, t % 2]).then_inc(inv_done, 1)
                t = s - S_AV
                if 0 <= t < NT:
                    dve.wait_ge(av_mm, t + 1)
                    dve.wait_ge(ld_xt[t % 4], 16 * (t // 4 + 1))
                    after(dve, t1b_done, t - 1)
                    v.tensor_tensor(t1[:, t % 2], av_p, xt[:, t % 4], ALU.add).then_inc(t1_done, 1)
                    dve.wait_ge(t1_done, t + 1)
                    v.bn_stats(bn1[:, t % 2], t1[:, t % 2]).then_inc(bn1_done, 1)
                    dve.wait_ge(bn1_done, t + 1)
                    after(dve, rstd1_done, t - 1)
                    v.bn_aggr(mv1[:, t % 2], bn1[:, t % 2]).then_inc(mv1_done, 1)
                t = s - S_SEL
                if 0 <= t < NT:
                    dve.wait_ge(ex_done, t + 1)
                    v.tensor_scalar(ex1[:, t % 2], ex[:, t % 2], 1.0, None, ALU.add).then_inc(ex1_done, 1)
                    dve.wait_ge(ex1_done, t + 1)
                    v.reciprocal(sig[:, t % 2], ex1[:, t % 2]).then_inc(sig_done, 1)
                    dve.wait_ge(sig_done, t + 1)
                    after(dve, cols_done, 2 * (t - 1))
                    v.max(top[:, t % 2], sig[:, t % 2]).then_inc(top_done, 1)
                    dve.wait_ge(top_done, t + 1)
                    v.max_index(topi[:, t % 2], top[:, t % 2], sig[:, t % 2]).then_inc(topi_done, 1)
                    dve.wait_ge(topi_done, t + 1)
                    v.tensor_copy(topf[:, t % 2], topi[:, t % 2, 0:2]).then_inc(topf_done, 1)
                    dve.wait_ge(topf_done, t + 1)
                    for r in range(2):
                        v.tensor_scalar(hot[:, t % 2, r], iota_e[:, :], topf[:, t % 2, r:r + 1], None,
                                        ALU.is_equal).then_inc(hot_done, 1)
                    dve.wait_ge(hot_done, 2 * t + 2)
                    after(dve, pos_mm, t - 1)
                    v.tensor_tensor(hotb[:, t % 2], hot[:, t % 2, 0], hot[:, t % 2, 1], ALU.add).then_inc(hotb_done, 1)
                t = s - S_AV
                if 0 <= t < NT:
                    dve.wait_ge(rstd1_done, t + 1)
                    after(dve, mix_mm, t - 1)
                    v.tensor_scalar(u1[:, t % 3], t1[:, t % 2], mv1[:, t % 2, 0:1], rstd1[:, t % 2, 1:2],
                                    ALU.subtract, ALU.mult).then_inc(u1_done, 1)
                t = s - S_MIX
                if 0 <= t < NT:
                    dve.wait_ge(h_mm, t + 1)
                    dve.wait_ge(t1b_done, t + 1)
                    v.tensor_tensor(t2[:, t], h_p, t1b[:, t % 2], ALU.add).then_inc(t2_done, 1)
                    dve.wait_ge(t2_done, t + 1)
                    v.bn_stats(bn2[:, t % 2], t2[:, t]).then_inc(bn2_done, 1)
                    dve.wait_ge(bn2_done, t + 1)
                    after(dve, rstd2_done, t - 1)
                    v.bn_aggr(mv2[:, t % 2], bn2[:, t % 2]).then_inc(mv2_done, 1)
                work = proj_work(s)
                if work:
                    for c in work[2]:
                        k_evac(work[0], c)
                    v_evac(work[0], work[1])
                if 0 <= t < NT:
                    dve.wait_ge(rstd2_done, t + 1)
                    after(dve, scattered[t % 4], 32 * (t // 4))
                    v.tensor_scalar(rows[:, t % 4, 0, 0:C], t2[:, t], mv2[:, t % 2, 0:1], rstd2[:, t % 2, 1:2],
                                    ALU.subtract, ALU.mult).then_inc(u2_done, 1)

            steps = [0]

            def planned(ins):
                steps[0] += 1
                ins.then_inc(plan, 1)
                dve.wait_ge(plan, steps[0])

            dve.wait_ge(cnt_mm, 1)
            planned(v.tensor_copy(cnt[:, :], cnt_p))
            planned(v.tensor_tensor(padr[:, :], cnt[:, :], ebase[:, :], ALU.add))
            v.tensor_copy(padr_i[:, :], padr[0:1, :]).then_inc(padr_done, 1)
            planned(v.tensor_scalar(tiles_i[:, :], cnt[:, :], 1.0 / P, (P - 1) / P - (P - 1) / (2 * P), ALU.mult, ALU.add))
            planned(v.tensor_copy(tiles_f[:, :], tiles_i[:, :]))
            planned(v.tensor_tensor_scan(tincl[:, :], ones_f[:, :], tiles_f[:, :], 0.0, ALU.mult, ALU.add))
            planned(v.tensor_tensor(texcl[:, :], tincl[:, :], tiles_f[:, :], ALU.subtract))
            planned(v.tensor_scalar(at_i[:, :], tincl[:, :], iota_p[:, 0:1], None, ALU.is_le))
            planned(v.tensor_scalar(at_x[:, :], texcl[:, :], iota_p[:, 0:1], None, ALU.is_le))
            planned(v.tensor_tensor(at_x[:, :], at_x[:, :], at_i[:, :], ALU.subtract))
            planned(v.scalar_tensor_tensor(out=rowt[:, :], in0=texcl[:, :], scalar=-float(P), in1=ebase[:, :],
                                           op0=ALU.mult, op1=ALU.add))
            planned(v.tensor_tensor_reduce(junk[:, 0, :], at_x[:, :], iota_e[:, :], 1.0, 0.0, ALU.mult, ALU.add, sums[:, 0:1]))
            planned(v.tensor_tensor_reduce(junk[:, 1, :], at_x[:, :], rowt[:, :], 1.0, 0.0, ALU.mult, ALU.add, sums[:, 1:2]))
            planned(v.tensor_scalar(used[:, :], at_i[:, NE - 1:NE], -1.0, 1.0, ALU.mult, ALU.add))
            planned(v.scalar_tensor_tensor(out=sched[:, 0:1], in0=at_i[:, NE - 1:NE], scalar=float(NE - 1), in1=sums[:, 0:1],
                                           op0=ALU.mult, op1=ALU.add))
            planned(v.scalar_tensor_tensor(out=term[:, 0:1], in0=i128[:, :], scalar=used[:, 0:1], in1=sums[:, 1:2],
                                           op0=ALU.mult, op1=ALU.add))
            v.scalar_tensor_tensor(out=sched[:, 1:2], in0=padr[:, NE - 1:NE], scalar=at_i[:, NE - 1:NE], in1=term[:, 0:1],
                                   op0=ALU.mult, op1=ALU.add).then_inc(sched_done, 1)
            dve.wait_ge(sched_mm, 1)
            v.tensor_copy(sched_i[:, :, :], sched_p.rearrange("p (a n) -> p a n", a=2)).then_inc(sched_out, 1)

            def round_(i):
                for g in range(2):
                    dve.wait_ge(ld_rows[g], i * (16 * GROUP) + 16 * GROUP)
                    after(dve, y_sent[g], i * (16 * GROUP))
                    v.tensor_copy(dest[:, g, :], xin[:, g, :, ID].bitcast(I32)).then_inc(cols_out, 1)
                    v.tensor_copy(wgt[:, g, :], xin[:, g, :, WEIGHT]).then_inc(cols_out, 1)
                    for q in range(2):
                        dve.wait_ge(H_mm, i * 4 + (2 * g + q + 1))
                        after(dve, HT_mm, i * 4 + 2 * g)
                        v.tensor_scalar(hid[:, 2 * q:2 * q + 2, 0:HID], H_p[q], 0.0, None, ALU.max).then_inc(hid_out, 1)
                    for q in range(2):
                        dve.wait_ge(HT_mm, i * 4 + (2 * g + q + 1))
                        after(dve, Y_mm, i * 4 + 2 * g)
                        v.tensor_copy(hT[:, 2 * q:2 * q + 2, :], HT_p[q][0:HID]).then_inc(HT_out, 1)
                    dve.wait_ge(Y_mm, i * 4 + (2 * g + 2))
                    for k in range(2, GROUP):
                        v.tensor_scalar(yb[:, g, k, :], Y_p[1][:, k - 2, :], wgt[:, g, k:k + 1], None, ALU.mult).then_inc(y_out_v, 1)

            round_(0)
            with dve.Fori(1, ITER) as i:
                round_(i)

            for c in range(NC_):
                dve.wait_ge(ld_pair[c % 2], 32 * (c // 2 + 1))
                t2c = t2[:, c * CG:(c + 1) * CG, :]
                v.tensor_tensor(t2c, t2c, pair0[:, c % 2], ALU.add).then_inc(half_sum, 1)
                dve.wait_ge(half_sum, c + 1)
                after(dve, stored[c % 2], 16 * (c // 2))
                v.tensor_tensor(fin[:, c % 2], t2c, pair1[:, c % 2], ALU.add).then_inc(out_sum, 1)

        @block.tensor
        def _(pe):
            m = nc.tensor

            def qk_proj(b, c):
                after(pe, v_out, v_evacs[0])
                after(pe, k_out, 2 * b + c)
                after(pe, q_out, 2 * b + c)
                for a in range(CH):
                    mm = m.matmul(bank7[:, :], wqk[:, a, :], xc[:, b % 2, a, c * 512:(c + 1) * 512],
                                  start=(a == 0), stop=(a == CH - 1))
                mm.then_inc(qk_mm, 1)
                qk_evacs[0] += 1

            def v_proj(b, j):
                after(pe, v_out, v_evacs[0])
                after(pe, k_out, qk_evacs[0])
                after(pe, q_out, qk_evacs[0])
                for a in range(CH):
                    mm = m.matmul(bank7[:, 0:C], xc[:, b % 2, a, j * P:(j + 1) * P], wv[:, a, :],
                                  start=(a == 0), stop=(a == CH - 1))
                mm.then_inc(v_mm, 1)
                v_evacs[0] += 1

            v_evacs, qk_evacs = [0], [0]
            pe.wait_ge(ld_wproj, 16 * 9)
            pe.wait_ge(ld_xc[0], 16)
            for c in range(2):
                qk_proj(0, c)
            for j in range(KB):
                v_proj(0, j)
            pe.wait_ge(const_done, 1)
            pe.wait_ge(ld_wmix, 48)

            for s in range(NT + LAST):
                t = s
                if t < NT:
                    b, tb = t // TB, t % TB
                    after(pe, centred, t)
                    pe.wait_ge(q_out, 2 * (b + 1))
                    pe.wait_ge(k_out, 2 * (b + 1))
                    for w in range(WT):
                        r = w // 2
                        rg = slice(r * QK, (r + 1) * QK)
                        for g in range(WT):
                            mm = m.matmul(E[g * H:(g + 1) * H, w * KB * W:(w + 1) * KB * W],
                                          q_s[rg, b % 2, (WT * tb + w) * H:(WT * tb + w + 1) * H],
                                          k_s[rg, b % 2, g].rearrange("p j v -> p (j v)"), start=True, stop=True)
                    mm.then_inc(e_mm, 1)
                t = s - S_MIX
                if 0 <= t < NT:
                    pe.wait_ge(u1_done, t + 1)
                    after(pe, uh_out, t)
                    tail = t % TB > 0
                    for a in range(CH):
                        cs = slice(a * P, (a + 1) * P)
                        m.transpose(mix_p[:, a, 0, :], u1[:, t % 3, cs], ident[:, :])
                        mm = m.matmul(mix_p[:, a, 1, :], u1[:, t % 3, cs], band[:, 0:P], start=True, stop=not tail)
                        if tail:
                            mm = m.matmul(mix_p[:, a, 1, 0:REACH], u1[P - REACH:P, (t - 1) % 3, cs],
                                          band[P - REACH:P, P:P + REACH], start=False, stop=True)
                    mm.then_inc(mix_mm, 1)
                t = s - S_SEL
                if 0 <= t < NT:
                    pe.wait_ge(u2_done, t + 1)
                    after(pe, u2T_out, t)
                    for a in range(CH):
                        mm = m.transpose(t2_p[:, a, :], rows[:, t % 4, 0, a * P:(a + 1) * P], ident[:, :])
                    mm.then_inc(u2T_mm, 1)
                t = s - S_POS
                if 0 <= t:
                    pe.wait_ge(hotb_done, t + 1)
                    after(pe, seen_done, t)
                    after(pe, spot_done, t)
                    pe.wait_ge(ex_done, min(t + S_POS - S_SEL, NT))
                    m.matmul(pos_p, upper[:, :], hotb[:, t % 2], start=True, stop=False)
                    m.matmul(pos_p, ones_b[:, :], seen[:, :], start=False, stop=True).then_inc(pos_mm, 1)
                t = s - S_AV
                if 0 <= t < NT:
                    b = t // TB
                    pe.wait_ge(prob_done, t + 1)
                    pe.wait_ge(v_out, (b + 1) * KB)
                    after(pe, t1_done, t)
                    pr = prob[:, t % 2].rearrange("p (j w) v -> p j (w v)", w=WT)
                    for j in range(KB):
                        mm = m.matmul(av_p, pr[:, j, :], vT[:, b % 2, j, :], start=(j == 0), stop=(j == KB - 1))
                    mm.then_inc(av_mm, 1)
                t = s - S_SEL
                if 0 <= t < NT:
                    pe.wait_ge(u2T_out, t + 1)
                    after(pe, ex_done, t)
                    after(pe, spot_done, t + S_SEL - S_POS + 1)
                    for a in range(CH):
                        mm = m.matmul(lg_p, u2T[:, t % 2, a, :], sels[:, a, :], start=(a == 0), stop=(a == CH - 1))
                    mm.then_inc(lg_mm, 1)
                t = s - S_MIX
                if 0 <= t < NT:
                    pe.wait_ge(uh_out, t + 1)
                    after(pe, t2_done, t)
                    for i, (side, a) in enumerate([(0, 0), (0, 1), (1, 0), (1, 1)]):
                        mm = m.matmul(h_p, uh[:, t % 2, a, side, :], (w1s, w2s)[side][:, a, :],
                                      start=(i == 0), stop=(i == 3))
                    mm.then_inc(h_mm, 1)
                work = proj_work(s)
                if work:
                    b, j, chunks = work
                    if j == 0:
                        pe.wait_ge(ld_xc[b % 2], 16 * (b // 2 + 1))
                    for c in chunks:
                        qk_proj(b, c)
                    v_proj(b, j)

            pe.wait_ge(seen_done, NT)
            m.matmul(cnt_p, ones_b[:, :], seen[:, :], start=True, stop=True).then_inc(cnt_mm, 1)
            pe.wait_ge(sched_done, 1)
            for c in range(2):
                mm = m.matmul(sched_p[:, c * P:(c + 1) * P], sched[:, c:c + 1], ident[:, :], start=True, stop=True)
            mm.then_inc(sched_mm, 1)
            pe.wait_ge(sched_out, 1)
            pe.wait_ge(ld_keys, 32)

            def round_(i):
                for g in range(2):
                    pe.wait_ge(ld_rows[g], i * (16 * GROUP) + 16 * GROUP)
                    after(pe, T_out, i * 4 + 2 * g)
                    for k in range(GROUP):
                        for a in range(CH):
                            mm = m.transpose(T_p[k // 2][:, k % 2, a, :], xin[:, g, k, a * P:(a + 1) * P], ident[:, :])
                        if k % 2:
                            mm.then_inc(T_mm, 1)
                    expert = [pe.value_load(sched_i[0:1, 0, bass.ds(i * (2 * GROUP) + (g * GROUP + k), 1)],
                                            min_val=0, max_val=NE - 1) for k in range(GROUP)]
                    after(pe, hid_out, i * 4 + 2 * g)
                    for k in range(GROUP):
                        if k % 2 == 0:
                            pe.wait_ge(T_out, i * 4 + (2 * g + k // 2 + 1))
                        for a in range(CH):
                            mm = m.matmul(H_p[k // 2][:, k % 2, :], uT[:, k, a, :], keys_s[:, a, bass.ds(expert[k], 1), :],
                                          start=(a == 0), stop=(a == CH - 1))
                        if k % 2:
                            mm.then_inc(H_mm, 1)
                    after(pe, HT_out, i * 4 + 2 * g)
                    for k in range(GROUP):
                        if k % 2 == 0:
                            pe.wait_ge(hid_out, i * 4 + (2 * g + k // 2 + 1))
                        mm = m.transpose(HT_p[k // 2][:, k % 2, :], hid[:, k, :], ident[:, :])
                        if k % 2:
                            mm.then_inc(HT_mm, 1)
                    after(pe, y_out_a, i * 4 + 2 * g)
                    after(pe, y_out_v, i * 4 + 2 * g)
                    for k in range(GROUP):
                        if k % 2 == 0:
                            pe.wait_ge(HT_out, i * 4 + (2 * g + k // 2 + 1))
                        mm = m.matmul(Y_p[k // 2][:, k % 2, :], hT[:, k, :], values_s[:, bass.ds(expert[k], 1), :],
                                      start=True, stop=True)
                        if k % 2:
                            mm.then_inc(Y_mm, 1)

            round_(0)
            with pe.Fori(1, ITER) as i:
                round_(i)


def kernel(**inputs):
    import numpy as np
    import concourse.bacc as bacc
    from concourse.bass_utils import run_bass_kernel_spmd

    a = {k: np.asarray(v) for k, v in inputs.items()}
    x = a["x"]
    laid = {
        "x_cm": x.transpose(1, 0, 3, 2).reshape(C, N),
        "x_tok": x.reshape(B, C, HW).transpose(0, 2, 1).reshape(N, C),
        "wqT": a["L0_conv_wq"].T,
        "bq": a["L0_conv_bq"].reshape(QK, 1),
        "wkT": a["L0_conv_wk"].T,
        "bk": a["L0_conv_bk"].reshape(QK, 1),
        "wvT": a["L0_conv_wv"].T,
        "bv": a["L0_conv_bv"].reshape(1, C),
        "gamma": a["L0_conv_gamma"].reshape(1, 1),
        "w1": a["L1_attn_W1"],
        "w2": a["L1_attn_W2"],
        "bias": a["L1_attn_bias"].reshape(1, C),
        "selT": a["L1_ffn_expert_sel"].T,
        "keys": a["L1_ffn_keys"].transpose(1, 0, 2),
        "values": a["L1_ffn_values"].transpose(1, 0, 2),
    }
    laid = {k: np.ascontiguousarray(v) for k, v in laid.items()}

    nc = bacc.Bacc("TRN2", target_bir_lowering=False, num_devices=1)
    args = [nc.dram_tensor(k, v.shape, mybir.dt.from_np(v.dtype), kind="ExternalInput").ap() for k, v in laid.items()]
    args.append(nc.dram_tensor("out", [N, C], F32, kind="ExternalOutput").ap())
    attention_moe(nc, *args)
    r = run_bass_kernel_spmd(nc, [laid], core_ids=[0])
    tokens = r.results[0]["out"]
    return tokens.reshape(B, HW, C).transpose(0, 2, 1).reshape(B, C, H, W)
```

```python
import concourse.bass as bass
from concourse import mybir
from contextlib import ExitStack
import itertools

F32 = mybir.dt.float32
BF16 = mybir.dt.bfloat16
I32 = mybir.dt.int32
U32 = mybir.dt.uint32
ALU = mybir.AluOpType
ACT = mybir.ActivationFunctionType
AX = mybir.AxisListType

P = 128
B, C, H, W = 4, 256, 32, 32
HW = H * W
N = B * HW
TB = HW // P
NT = N // P
CH = C // P
QK = C // 8
WT = P // H
KB = W // WT
REACH = 32
NE, HID = 32, 64
CAP = N + P
ROW = C + 2
ID, WEIGHT = C, C + 1
SLOT_TILES = 2 * N // P + NE
GROUP = 4
NB = 4
BLK = 8
LN_EPS = 1e-5
PB = NE * (P // BLK) // P
PR = NE * BLK // P
WARM = 40
PADROW = 2 * N

S_AV, S_MIX, S_NORM2, S_ROUTE, S_POS = 1, 2, 3, 4, 5
LAST = S_POS


def attention_moe(nc, x_cm, x_tok, wqT, bq, wkT, bk, wvT, bv, gamma, w1, w2, bias, selT, keys, values, out):
    slots_d = nc.dram_tensor("slot_rows", [NE * CAP + P, ROW], F32, kind="Internal").ap()
    pair_d = nc.dram_tensor("expert_outputs", [2 * N, C], F32, kind="Internal").ap()

    with ExitStack() as ctx:
        def sb(name, shape, dt=F32):
            return ctx.enter_context(nc.sbuf_tensor(name, shape, dt))

        def ps(name, shape, dt=F32):
            return ctx.enter_context(nc.psum_tensor(name, shape, dt))

        def sem(name):
            return ctx.enter_context(nc.semaphore(name))

        wqk = sb("wqk", [P, CH, 2 * QK])
        bqk = sb("bqk", [2 * QK, 1])
        wv = sb("wv", [P, CH, C])
        gbv = sb("gbv", [P, C])
        gam = sb("gam", [P, 1])
        w1s = sb("w1s", [P, CH, C])
        w2s = sb("w2s", [P, CH, C])
        biasb = sb("biasb", [P, C])
        sels = sb("sels", [P, CH, NE])
        keys_s = sb("keys_s", [P, CH, NE, HID])
        values_s = sb("values_s", [HID, NE, C])
        ident = sb("ident", [P, P])
        band = sb("band", [P, P + REACH])
        upper = sb("upper", [P, P], BF16)
        ones_b = sb("ones_b", [P, P], BF16)
        ones_f = sb("ones_f", [P, NE])
        iota_e = sb("iota_e", [P, NE])
        ebase = sb("ebase", [P, NE])
        iota_p = sb("iota_p", [P, 1])
        out_ids = sb("out_ids", [P, NT, 2], I32)
        pad_rows = sb("pad_rows", [P, BLK, ROW])
        half_neg = sb("half_neg", [P, 1])

        xc_or_xin = sb("xc_or_xin", [P, max(2 * CH * HW, NB * GROUP * ROW)])
        xc = xc_or_xin[:, 0:2 * CH * HW].rearrange("p (b a n) -> p b a n", b=2, a=CH)
        q_s = sb("q_s", [P, W, WT, H])
        k_s = sb("k_s", [P, 2, KB, W])
        vT = sb("vT", [P, 2, KB, C])
        xt = sb("xt", [P, 4, C])
        prob = sb("prob", [P, 2, KB * WT, W])
        gmax = sb("gmax", [P, 2, WT * KB])
        gsum = sb("gsum", [P, 2, WT * KB])
        ginv = sb("ginv", [P, 2, WT * KB])
        t1 = sb("t1", [P, 2, C])
        t1b = sb("t1b", [P, 2, C])
        bn1 = sb("bn1", [P, 2, 6])
        mv1 = sb("mv1", [P, 2, 2])
        rstd1 = sb("rstd1", [P, 2, 3])
        u1 = sb("u1", [P, 3, C])
        uh = sb("uh", [P, 2, CH, 2, P])
        t2 = sb("t2", [P, NT, C])
        bn2 = sb("bn2", [P, 2, 6])
        mv2 = sb("mv2", [P, 2, 2])
        rstd2 = sb("rstd2", [P, 2, 3])
        rows = sb("rows", [P, 4, 2, ROW])
        u2T = sb("u2T", [P, 2, CH, P])
        ex = sb("ex", [P, 2, NE])
        ex1 = sb("ex1", [P, 2, NE])
        sig = sb("sig", [P, 2, NE])
        top = sb("top", [P, 2, 8])
        topi = sb("topi", [P, 2, 8], U32)
        topf = sb("topf", [P, 2, 2])
        hot = sb("hot", [P, 2, 2, NE])
        hotb = sb("hotb", [P, 2, NE], BF16)
        seen = sb("seen", [P, NE], BF16)
        spot = sb("spot", [P, 2, NE])
        picked = sb("picked", [P, 2, 2, NE])
        slotf = sb("slotf", [P, 2, 2])
        slot = sb("slot", [P, 4, 2], I32)

        cnt = sb("cnt", [P, NE])
        tiles_i = sb("tiles_i", [P, NE], I32)
        tiles_f = sb("tiles_f", [P, NE])
        tincl = sb("tincl", [P, NE])
        texcl = sb("texcl", [P, NE])
        at_i = sb("at_i", [P, NE])
        at_x = sb("at_x", [P, NE])
        rowt = sb("rowt", [P, NE])
        padr = sb("padr", [P, NE])
        blk_f = sb("blk_f", [P, NE])
        blk_i = sb("blk_i", [P, NE], I32)
        pick_b = sb("pick_b", [P, PB, NE])
        pick_r = sb("pick_r", [P, PR, NE])
        off_b = sb("off_b", [P, PB])
        off_r = sb("off_r", [P, PR])
        tmp_b = sb("tmp_b", [P, 2, PB, NE])
        tmp_r = sb("tmp_r", [P, 2, PR, NE])
        ends = sb("ends", [P, 4, NE])
        ebase_b = sb("ebase_b", [P, 2, NE])
        eoff_r = sb("eoff_r", [P, NE])
        pad_b = sb("pad_b", [P, 2, PB])
        pad_r = sb("pad_r", [P, 2, PR])
        over_b = sb("over_b", [P, PB])
        over_r = sb("over_r", [P, PR])
        pad_b_i = sb("pad_b_i", [P, PB], I32)
        pad_r_i = sb("pad_r_i", [P, PR], I32)
        sched = sb("sched", [P, 2])
        sums = sb("sums", [P, 2])
        i128 = sb("i128", [P, 1])
        used = sb("used", [P, 1])
        term = sb("term", [P, 2])
        junk = sb("junk", [P, 2, NE])
        sched_i = sb("sched_i", [1, 2, P], I32)

        xin = xc_or_xin[:, 0:NB * GROUP * ROW].rearrange("p (b k r) -> p b k r", b=NB, k=GROUP)
        dest = sb("dest", [P, NB, GROUP], I32)
        wgt = sb("wgt", [P, NB, GROUP])
        uT = uh[:, :, :, :, :].rearrange("p b a s n -> p (b a) s n")
        hid = sb("hid", [P, GROUP, P])
        hT = q_s[0:HID, 0:W // 4].rearrange("p w g h -> p (w g h)").rearrange("p (b k n) -> p b k n", b=2, k=GROUP)
        yb = vT[:, :, :, :].rearrange("p a (b k) n -> p (a b) k n", k=GROUP)

        E = ps("E", [P, WT * KB * W])
        bank = {i: ps(f"bank{i}", [P, 512]) for i in range(2, 8)}
        av_p = bank[2][:, 0:C]
        mix_p = bank[3][:, :].rearrange("p (a s n) -> p a s n", a=CH, s=2)
        h_p = bank[4][:, 0:C]
        t2_p = bank[5][:, 0:C].rearrange("p (a n) -> p a n", a=CH)
        lg_p = bank[6][:, 0:NE]
        pos_p = bank[6][:, NE:2 * NE]
        bank7 = bank[7]
        cnt_p = bank[6][:, 0:NE]
        sched_p = bank[2][0:1, 0:2 * P]
        T_p = [E[:, q * 512:(q + 1) * 512].rearrange("p (k a n) -> p k a n", k=2, a=CH) for q in range(2)]
        H_p = [bank[2 + q][:, 0:2 * HID].rearrange("p (k n) -> p k n", k=2) for q in range(2)]
        HT_p = [bank[4 + q][:, 0:2 * P].rearrange("p (k n) -> p k n", k=2) for q in range(2)]
        Y_p = [bank[6 + q][:, :].rearrange("p (k n) -> p k n", k=2) for q in range(2)]

        ld_wproj, ld_wmix, ld_bcast, ld_keys = sem("ld_wproj"), sem("ld_wmix"), sem("ld_bcast"), sem("ld_keys")
        ld_xc = [sem(f"ld_xc{i}") for i in range(2)]
        ld_xt = [sem(f"ld_xt{i}") for i in range(4)]
        pick_step, q_zero, spare_done = sem("pick_step"), sem("q_zero"), sem("spare_done")
        const_raw, const_done, gbv_done = sem("const_raw"), sem("const_done"), sem("gbv_done")
        qk_mm, q_out, k_out, v_mm, v_out = sem("qk_mm"), sem("q_out"), sem("k_out"), sem("v_mm"), sem("v_out")
        e_mm, max_done, centred, exp_done = sem("e_mm"), sem("max_done"), sem("centred"), sem("exp_done")
        sum_done, inv_done, prob_done, av_mm = sem("sum_done"), sem("inv_done"), sem("prob_done"), sem("av_mm")
        t1_done, bn1_done, mv1_done, ve1_done = sem("t1_done"), sem("bn1_done"), sem("mv1_done"), sem("ve1_done")
        rstd1_done, u1_done, t1b_done = sem("rstd1_done"), sem("u1_done"), sem("t1b_done")
        mix_mm, uh_out, h_mm, t2_done = sem("mix_mm"), sem("uh_out"), sem("h_mm"), sem("t2_done")
        bn2_done, mv2_done, ve2_done, rstd2_done = sem("bn2_done"), sem("mv2_done"), sem("ve2_done"), sem("rstd2_done")
        u2_done, u2_copied, u2T_mm, u2T_out = sem("u2_done"), sem("u2_copied"), sem("u2T_mm"), sem("u2T_out")
        lg_mm, ex_done, ex1_done, sig_done = sem("lg_mm"), sem("ex_done"), sem("ex1_done"), sem("sig_done")
        top_done, topi_done, topf_done, hot_done = sem("top_done"), sem("topi_done"), sem("topf_done"), sem("hot_done")
        hotb_done, pos_mm, seen_done, spot_done = sem("hotb_done"), sem("pos_mm"), sem("seen_done"), sem("spot_done")
        slotf_done, slot_done, cols_done = sem("slotf_done"), sem("slot_done"), sem("cols_done")
        scattered = [sem(f"scattered{i}") for i in range(4)]
        cnt_mm, plan, padr_done = sem("cnt_mm"), sem("plan"), sem("padr_done")
        sched_done, sched_mm, sched_out, pads_filled = sem("sched_done"), sem("sched_mm"), sem("sched_out"), sem("pads_filled")
        ld_rows = [sem(f"ld_rows{i}") for i in range(NB)]
        nmr1_done, nmr2_done, pads_done = sem("nmr1_done"), sem("nmr2_done"), sem("pads_done")
        cols_out, T_mm, T_out, H_mm, hid_out = sem("cols_out"), sem("T_mm"), sem("T_out"), sem("H_mm"), sem("hid_out")
        HT_mm, HT_out, Y_mm, y_out_a, y_out_v = sem("HT_mm"), sem("HT_out"), sem("Y_mm"), sem("y_out_a"), sem("y_out_v")
        y_sent = [sem(f"y_sent{i}") for i in range(NB)]
        ld_pair = [sem(f"ld_pair{i}") for i in range(2)]
        half_sum, out_sum = sem("half_sum"), sem("out_sum")
        stored = [sem(f"stored{i}") for i in range(2)]

        def after(eng, s, n):
            if not isinstance(n, int) or n > 0:
                eng.wait_ge(s, n)

        def computed(eng, value):
            if isinstance(value, int):
                return value
            reg = eng.alloc_register(f"wait_value_{next(number)}")
            eng.reg_mov(reg, value)
            return eng.snap(reg)

        def loaded(eng, regs, words, largest):
            eng.reg_load(regs, words)
            return [eng.snap(r, min_val=0, max_val=largest) for r in regs]

        number = itertools.count()
        ITER = SLOT_TILES // (NB * GROUP)

        def over_groups(eng, step):
            for g in range(NB):
                step(0, g, g == 0, False)
            with eng.Fori(1, ITER - 1) as i:
                for g in range(NB):
                    step(i, g, False, False)
            for g in range(NB):
                step(ITER - 1, g, False, g == NB - 1)

        def following(i, g):
            return (i, g + 1) if g < NB - 1 else (i + 1, 0)

        def pairs(i, g):
            return i * (2 * NB) + 2 * g

        def dma_count(i):
            return i * (16 * GROUP)
        CG = 4
        NC_ = NT // CG
        fin = prob[:, :, :, :].rearrange("p a b c -> p a (b c)").rearrange("p a (t n) -> p a t n", n=C)
        pair0 = yb[:, 0:2]
        pair1 = xc[:, 0, :, :].rearrange("p a n -> p (a n)").rearrange("p (a t n) -> p a t n", a=2, n=C)

        def proj_work(s):
            b, j = s // TB + 1, s % TB
            if b >= B:
                return None
            return b, j, ([j - (TB - 2)] if j >= TB - 2 else [])

        def v_no(b, j):
            return b * KB + j

        block = ctx.enter_context(nc.Block())

        @block.sync
        def _(sp):
            half = "(a p) n -> p a n"
            sp.dma_start(xc[:, 0, :, :], x_cm[:, 0:HW].rearrange(half, p=P)).then_inc(ld_xc[0], 16)
            sp.dma_start(wqk[:, :, 0:QK], wqT.rearrange(half, p=P)).then_inc(ld_wproj, 16)
            sp.dma_start(wqk[:, :, QK:2 * QK], wkT.rearrange(half, p=P)).then_inc(ld_wproj, 16)
            sp.dma_start(bqk[0:QK, :], bq).then_inc(ld_wproj, 16)
            sp.dma_start(bqk[QK:2 * QK, :], bk).then_inc(ld_wproj, 16)
            sp.dma_start(wv[:, :, :], wvT.rearrange(half, p=P)).then_inc(ld_wproj, 16)
            sp.dma_start(gbv[:, :], bv.to_broadcast([P, C])).then_inc(ld_bcast, 16)
            sp.dma_start(gam[:, :], gamma.to_broadcast([P, 1])).then_inc(ld_bcast, 16)
            sp.dma_start(biasb[:, :], bias.to_broadcast([P, C])).then_inc(ld_bcast, 16)
            sp.dma_start(xc[:, 1, :, :], x_cm[:, HW:2 * HW].rearrange(half, p=P)).then_inc(ld_xc[1], 16)
            sp.dma_start(w1s[:, :, :], w1.rearrange(half, p=P)).then_inc(ld_wmix, 16)
            sp.dma_start(w2s[:, :, :], w2.rearrange(half, p=P)).then_inc(ld_wmix, 16)
            sp.dma_start(sels[:, :, :], selT.rearrange(half, p=P)).then_inc(ld_wmix, 16)
            for t in range(NT):
                if t == 4:
                    sp.dma_start(keys_s[:, :, :, :], keys.rearrange("(a p) e h -> p a e h", p=P)).then_inc(ld_keys, 16)
                    sp.dma_start(values_s[:, :, :], values).then_inc(ld_keys, 16)
                if t >= 4:
                    sp.wait_ge(t1_done, t - 3)
                sp.dma_start(xt[:, t % 4, :], x_tok[t * P:(t + 1) * P, :]).then_inc(ld_xt[t % 4], 16)
                b = t // TB + 2
                if t % TB == 4 and 2 <= b < B:
                    sp.wait_ge(v_mm, v_no(b - 2, KB - 1) + 1)
                    sp.wait_ge(qk_mm, 2 * (b - 1))
                    sp.dma_start(xc[:, b % 2, :, :],
                                 x_cm[:, b * HW:(b + 1) * HW].rearrange(half, p=P)).then_inc(ld_xc[b % 2], 16)

            sp.wait_ge(const_done, 1)
            sp.dma_start(slots_d[NE * CAP:NE * CAP + P, :], pad_rows[:, 0, :]).then_inc(spare_done, 16)
            sp.wait_ge(spare_done, 16)
            sp.wait_ge(pads_done, 16 * (PB + PR))
            for i in range(4):
                sp.wait_ge(scattered[i], 2 * 16 * (NT // 4))
            sp.wait_ge(sched_out, 1)

            starts = [sp.alloc_register(f"start{k}") for k in range(GROUP)]

            def load_group(i, g, first, last):
                start = loaded(sp, starts, sched_i[0:1, 1, bass.ds(i * (NB * GROUP) + g * GROUP, GROUP)], NE * CAP)
                done = computed(sp, pairs(i, g) - 2 * NB + 2)
                sp.wait_ge(sched_out, 1)
                if not (isinstance(i, int) and i == 0):
                    sp.wait_ge(T_mm, done)
                    sp.wait_ge(cols_out, done)
                for k in range(GROUP):
                    sp.dma_start(xin[:, g, k, :], slots_d[bass.ds(start[k], P), :]).then_inc(ld_rows[g], 16)

            over_groups(sp, load_group)

            for g in range(NB):
                sp.wait_ge(y_sent[g], 16 * SLOT_TILES // NB)
            for c in range(NC_):
                if c >= 2:
                    sp.wait_ge(out_sum, c - 1)
                for r, buf in enumerate((pair0, pair1)):
                    src = pair_d[r * N + c * CG * P:r * N + (c + 1) * CG * P, :]
                    sp.dma_start(buf[:, c % 2, :, :], src.rearrange("(t p) n -> p t n", p=P)).then_inc(ld_pair[c % 2], 16)

        @block.gpsimd
        def _(pool):
            g = nc.gpsimd
            g.memset(q_s[:, :, :, :], 0.0).then_inc(q_zero, 1)
            g.memset(ident[:, :], 0.0).then_inc(const_raw, 1)
            g.memset(upper[:, :], 1.0).then_inc(const_raw, 1)
            g.iota(band[:, :], pattern=[[1, P + REACH]], base=0, channel_multiplier=-1,
                   allow_small_or_imprecise_dtypes=True).then_inc(const_raw, 1)
            g.memset(pad_rows[:, :, :], 0.0).then_inc(const_raw, 1)
            g.memset(half_neg[:, :], -0.5)
            g.memset(ones_b[:, :], 1.0)
            g.memset(ones_f[:, :], 1.0)
            g.memset(seen[:, :], 0.0)
            g.memset(hid[:, :, :], 0.0)
            g.iota(iota_e[:, :], pattern=[[1, NE]], base=0, channel_multiplier=0, allow_small_or_imprecise_dtypes=True)
            g.iota(ebase[:, :], pattern=[[CAP, NE]], base=0, channel_multiplier=0, allow_small_or_imprecise_dtypes=True)
            g.iota(iota_p[:, :], pattern=[[0, 1]], base=0, channel_multiplier=1, allow_small_or_imprecise_dtypes=True)
            g.iota(i128[:, :], pattern=[[0, 1]], base=0, channel_multiplier=P, allow_small_or_imprecise_dtypes=True)
            for cols, pick, per in ((PB, pick_b, P // BLK), (PR, pick_r, BLK)):
                g.memset(pick[:, :, :], 1.0).then_inc(pick_step, 1)
            for n, (cols, pick, per) in enumerate(((PB, pick_b, P // BLK), (PR, pick_r, BLK))):
                pool.wait_ge(pick_step, 2 + 2 * n)
                g.affine_select(out=pick[:, :, :], in_=pick[:, :, :], compare_op=ALU.is_ge, fill=0.0, base=0,
                                pattern=[[P, cols], [-per, NE]], channel_multiplier=1).then_inc(pick_step, 1)
                pool.wait_ge(pick_step, 3 + 2 * n)
                g.affine_select(out=pick[:, :, :], in_=pick[:, :, :], compare_op=ALU.is_ge, fill=0.0, base=per - 1,
                                pattern=[[-P, cols], [per, NE]], channel_multiplier=-1).then_inc(pick_step, 1)
            g.iota(ebase_b[:, 0, :], pattern=[[CAP // BLK - P // BLK, NE]], base=0, channel_multiplier=0,
                   allow_small_or_imprecise_dtypes=True)
            g.iota(ebase_b[:, 1, :], pattern=[[CAP // BLK, NE]], base=0, channel_multiplier=0,
                   allow_small_or_imprecise_dtypes=True)
            g.iota(eoff_r[:, :], pattern=[[-BLK, NE]], base=0, channel_multiplier=0, allow_small_or_imprecise_dtypes=True)
            g.iota(off_b[:, :], pattern=[[P, PB]], base=0, channel_multiplier=1, allow_small_or_imprecise_dtypes=True)
            g.iota(off_r[:, :], pattern=[[P, PR]], base=0, channel_multiplier=1, allow_small_or_imprecise_dtypes=True)
            g.iota(out_ids[:, :, :], pattern=[[P, NT], [N, 2]], base=0, channel_multiplier=1).then_inc(const_raw, 1)
            pool.wait_ge(const_raw, 5)
            g.affine_select(out=ident[:, :], in_=ident[:, :], compare_op=ALU.not_equal, fill=1.0, base=0,
                            pattern=[[-1, P]], channel_multiplier=1).then_inc(const_raw, 1)
            g.affine_select(out=upper[:, :], in_=upper[:, :], compare_op=ALU.is_gt, fill=0.0, base=0,
                            pattern=[[1, P]], channel_multiplier=-1).then_inc(const_raw, 1)
            g.affine_select(out=band[:, :], in_=band[:, :], compare_op=ALU.is_gt, fill=0.0, base=0,
                            pattern=[[1, P + REACH]], channel_multiplier=-1).then_inc(const_raw, 1)
            g.iota(pad_rows[:, :, ID].bitcast(I32), pattern=[[1, BLK]], base=PADROW,
                   channel_multiplier=BLK).then_inc(const_raw, 1)
            pool.wait_ge(const_raw, 9)
            g.affine_select(out=band[:, :], in_=band[:, :], compare_op=ALU.is_ge, fill=0.0, base=REACH,
                            pattern=[[-1, P + REACH]], channel_multiplier=1).then_inc(const_done, 1)

            def layer_norm_factors(t, mv, mv_done, rstd, used, ve_done, rstd_done, nmr_done):
                pool.wait_ge(mv_done, t + 1)
                after(pool, used, t - 1)
                g.tensor_scalar(rstd[:, t % 2, 0:1], mv[:, t % 2, 1:2], LN_EPS, None, ALU.add).then_inc(ve_done, 1)
                pool.wait_ge(ve_done, t + 1)
                g.tensor_tensor(rstd[:, t % 2, 1:2], rstd[:, t % 2, 0:1], half_neg[:, :], ALU.pow).then_inc(rstd_done, 1)
                pool.wait_ge(rstd_done, t + 1)
                g.tensor_scalar(rstd[:, t % 2, 2:3], mv[:, t % 2, 0:1], rstd[:, t % 2, 1:2], -1.0,
                                ALU.mult, ALU.mult).then_inc(nmr_done, 1)

            for s in range(NT + LAST):
                t = s - S_NORM2
                if 0 <= t < NT:
                    layer_norm_factors(t, mv2, mv2_done, rstd2, u2_copied, ve2_done, rstd2_done, nmr2_done)
                t = s - S_POS
                if 0 <= t:
                    pool.wait_ge(slot_done, t + 1)
                    pool.wait_ge(u2_copied, t + 1)
                    g.tensor_copy(rows[:, t % 4, :, ID].bitcast(I32), out_ids[:, t, :]).then_inc(cols_done, 1)
                    g.tensor_copy(rows[:, t % 4, :, WEIGHT], top[:, t % 2, 0:2]).then_inc(cols_done, 1)
                    pool.wait_ge(cols_done, 2 * t + 2)
                    for r in range(2):
                        g.indirect_dma_start(
                            out=slots_d, out_offset=bass.IndirectOffsetOnAxis(ap=slot[:, t % 4, r:r + 1], axis=0),
                            in_=rows[:, t % 4, r, :], in_offset=None).then_inc(scattered[t % 4], 16)
                t = s
                if t < NT:
                    pool.wait_ge(inv_done, t + 1)
                    g.tensor_tensor(prob[:, t % 2], prob[:, t % 2],
                                    ginv[:, t % 2].unsqueeze(2).to_broadcast([P, WT * KB, W]),
                                    ALU.mult).then_inc(prob_done, 1)
                t = s - S_AV
                if 0 <= t < NT:
                    layer_norm_factors(t, mv1, mv1_done, rstd1, u1_done, ve1_done, rstd1_done, nmr1_done)
                    after(pool, t2_done, t - 1)
                    if t == 0:
                        pool.wait_ge(ld_bcast, 48)
                    g.tensor_tensor(t1b[:, t % 2], t1[:, t % 2], biasb[:, :], ALU.add).then_inc(t1b_done, 1)

            pool.wait_ge(padr_done, 2)
            blocks_d = slots_d.rearrange("(n k) c -> n (k c)", k=BLK)
            for c in range(PB):
                g.indirect_dma_start(
                    out=blocks_d, out_offset=bass.IndirectOffsetOnAxis(ap=pad_b_i[:, c:c + 1], axis=0),
                    in_=pad_rows[:, :, :].rearrange("p k c -> p (k c)"), in_offset=None,
                    bounds_check=NE * CAP // BLK - 1, oob_is_err=False).then_inc(pads_done, 16)
            for c in range(PR):
                g.indirect_dma_start(
                    out=slots_d, out_offset=bass.IndirectOffsetOnAxis(ap=pad_r_i[:, c:c + 1], axis=0),
                    in_=pad_rows[:, 0, :], in_offset=None,
                    bounds_check=NE * CAP - 1, oob_is_err=False).then_inc(pads_done, 16)

            def send_group(i, gr):
                copied = computed(pool, pairs(i, gr) + 2)
                for k in range(GROUP):
                    weighted = computed(pool, pairs(i, gr) + (k % 2 + 1))
                    pool.wait_ge(sched_out, 1)
                    pool.wait_ge(cols_out, copied)
                    pool.wait_ge(y_out_a if k < 2 else y_out_v, weighted)
                    g.indirect_dma_start(
                        out=pair_d, out_offset=bass.IndirectOffsetOnAxis(ap=dest[:, gr, k:k + 1], axis=0),
                        in_=yb[:, gr, k, :], in_offset=None,
                        bounds_check=2 * N - 1, oob_is_err=False).then_inc(y_sent[gr], 16)

            over_groups(pool, lambda i, gr, first, last: send_group(i, gr))

        @block.scalar
        def _(act):
            a = nc.scalar

            def q_evac(b, c):
                act.wait_ge(qk_mm, 2 * b + c + 1)
                after(act, e_mm, TB * (b - 1) + (c + 1) * TB // 2)
                if b == 0:
                    act.wait_ge(q_zero, 1)
                for g in range(WT):
                    qa = a.activation(q_s[g * QK:(g + 1) * QK, c * W // 2:(c + 1) * W // 2, g, :],
                                      bank7[0:QK, :].rearrange("p (w h) -> p w h", h=H), ACT.Identity,
                                      bias=bqk[0:QK, 0:1])
                qa.then_inc(q_out, 1)

            for c in range(2):
                q_evac(0, c)
            for s in range(NT + LAST):
                t = s
                if t < NT:
                    act.wait_ge(centred, t + 1)
                    a.activation(prob[:, t % 2], prob[:, t % 2], ACT.Exp).then_inc(exp_done, 1)
                t = s - S_MIX
                if 0 <= t < NT:
                    act.wait_ge(mix_mm, t + 1)
                    after(act, h_mm, t - 1)
                    a.activation(uh[:, t % 2], mix_p, ACT.Copy).then_inc(uh_out, 1)
                t = s - S_NORM2
                if 0 <= t < NT:
                    act.wait_ge(nmr2_done, t + 1)
                    after(act, scattered[t % 4], 32 * (t // 4))
                    for r, done in enumerate((u2_done, u2_copied)):
                        a.activation(rows[:, t % 4, r, 0:C], t2[:, t], ACT.Identity, bias=rstd2[:, t % 2, 2:3],
                                     scale=rstd2[:, t % 2, 1:2]).then_inc(done, 1)
                    act.wait_ge(u2T_mm, t + 1)
                    after(act, lg_mm, t - 1)
                    a.activation(u2T[:, t % 2], t2_p, ACT.Copy).then_inc(u2T_out, 1)
                t = s - S_AV
                if 0 <= t < NT:
                    act.wait_ge(nmr1_done, t + 1)
                    after(act, mix_mm, t - 1)
                    a.activation(u1[:, t % 3], t1[:, t % 2], ACT.Identity, bias=rstd1[:, t % 2, 2:3],
                                 scale=rstd1[:, t % 2, 1:2]).then_inc(u1_done, 1)
                t = s - S_NORM2
                if 0 <= t < NT:
                    act.wait_ge(lg_mm, t + 1)
                    after(act, ex1_done, t - 1)
                    a.activation(ex[:, t % 2], lg_p, ACT.Exp, scale=-1.0).then_inc(ex_done, 1)
                work = proj_work(s)
                if work:
                    for c in work[2]:
                        q_evac(work[0], c)

            def transposed(i, g):
                for q in range(2):
                    act.wait_ge(T_mm, pairs(i, g) + (q + 1))
                    after(act, H_mm, pairs(i, g))
                    a.activation(uT[:, 2 * q:2 * q + 2], T_p[q], ACT.Copy).then_inc(T_out, 1)

            def weighted(i, g):
                after(act, y_sent[g], dma_count(i))
                act.wait_ge(cols_out, pairs(i, g) + 2)
                act.wait_ge(Y_mm, pairs(i, g) + 1)
                for k in range(2):
                    a.activation(yb[:, g, k, :], Y_p[0][:, k, :], ACT.Copy, scale=wgt[:, g, k:k + 1]).then_inc(y_out_a, 1)

            def act_group(i, g, first, last):
                if not last:
                    transposed(*following(i, g))
                weighted(i, g)

            transposed(0, 0)
            over_groups(act, act_group)

            for c in range(NC_):
                act.wait_ge(out_sum, c + 1)
                rows_out = out[c * CG * P:(c + 1) * CG * P, :].rearrange("(t p) n -> p t n", p=P)
                act.dma_start(rows_out, fin[:, c % 2]).then_inc(stored[c % 2], 16)
            for i in range(2):
                act.wait_ge(stored[i], 16 * (NC_ // 2))

        @block.vector
        def _(dve):
            v = nc.vector

            def k_evac(b, c):
                dve.wait_ge(qk_mm, 2 * b + c + 1)
                after(dve, e_mm, TB * (b - 1))
                for g in range(WT):
                    src = bank7[QK:2 * QK, :].rearrange("p (v j g) -> p g j v", g=WT, j=KB)[:, g]
                    ka = v.tensor_scalar(k_s[g * QK:(g + 1) * QK, b % 2, :, c * W // 2:(c + 1) * W // 2], src,
                                         bqk[QK:2 * QK, 0:1], None, ALU.add)
                ka.then_inc(k_out, 1)

            def v_evac(b, j):
                dve.wait_ge(v_mm, v_no(b, j) + 1)
                after(dve, av_mm, TB * (b - 1))
                v.scalar_tensor_tensor(out=vT[:, b % 2, j, :], in0=bank7[:, 0:C], scalar=gam[:, 0:1], in1=gbv[:, :],
                                       op0=ALU.mult, op1=ALU.add).then_inc(v_out, 1)

            dve.wait_ge(ld_bcast, 48)
            v.tensor_scalar(gbv[:, :], gbv[:, :], gam[:, 0:1], None, ALU.mult).then_inc(gbv_done, 1)
            dve.wait_ge(ld_wproj, 16 * 5)
            for c in range(2):
                k_evac(0, c)
            dve.wait_ge(gbv_done, 1)
            for j in range(KB):
                v_evac(0, j)
            dve.wait_ge(const_done, 1)

            for s in range(NT + LAST):
                t, t1_, t2_, tr, tp = s, s - S_AV, s - S_NORM2, s - S_ROUTE, s - S_POS
                soft, res1, res2 = t < NT, 0 <= t1_ < NT, 0 <= t2_ < NT
                route, place = 0 <= tr < NT, 0 <= tp < NT
                work = proj_work(s)
                if res2:
                    dve.wait_ge(h_mm, t2_ + 1)
                    dve.wait_ge(t1b_done, t2_ + 1)
                    v.tensor_tensor(t2[:, t2_], h_p, t1b[:, t2_ % 2], ALU.add).then_inc(t2_done, 1)
                if soft:
                    dve.wait_ge(e_mm, t + 1)
                    v.tensor_reduce(gmax[:, t % 2], E[:, :].rearrange("p (a v) -> p a v", v=W),
                                    AX.X, ALU.max).then_inc(max_done, 1)
                if res2:
                    dve.wait_ge(t2_done, t2_ + 1)
                    v.bn_stats(bn2[:, t2_ % 2], t2[:, t2_]).then_inc(bn2_done, 1)
                if soft:
                    dve.wait_ge(max_done, t + 1)
                    after(dve, av_mm, t - 1)
                    v.tensor_tensor(prob[:, t % 2].rearrange("p (j w) v -> p w j v", w=WT),
                                    E[:, :].rearrange("p (w j v) -> p w j v", w=WT, v=W),
                                    gmax[:, t % 2].rearrange("p (w j) -> p w j", w=WT).unsqueeze(3)
                                    .to_broadcast([P, WT, KB, W]), ALU.subtract).then_inc(centred, 1)
                if res2:
                    dve.wait_ge(bn2_done, t2_ + 1)
                    after(dve, nmr2_done, t2_ - 1)
                    v.bn_aggr(mv2[:, t2_ % 2], bn2[:, t2_ % 2]).then_inc(mv2_done, 1)
                if route:
                    dve.wait_ge(ex_done, tr + 1)
                    v.tensor_scalar(ex1[:, tr % 2], ex[:, tr % 2], 1.0, None, ALU.add).then_inc(ex1_done, 1)
                if place:
                    dve.wait_ge(pos_mm, tp + 1)
                    v.tensor_tensor(spot[:, tp % 2], pos_p, ebase[:, :], ALU.add).then_inc(spot_done, 1)
                if route:
                    dve.wait_ge(ex1_done, tr + 1)
                    v.reciprocal(sig[:, tr % 2], ex1[:, tr % 2]).then_inc(sig_done, 1)
                if place:
                    dve.wait_ge(spot_done, tp + 1)
                    v.tensor_tensor_reduce(picked[:, tp % 2, 0], hot[:, tp % 2, 0], spot[:, tp % 2], 1.0, 0.0,
                                           ALU.mult, ALU.add, slotf[:, tp % 2, 0:1]).then_inc(slotf_done, 1)
                if route:
                    dve.wait_ge(sig_done, tr + 1)
                    after(dve, cols_done, 2 * (tr - 1))
                    v.max(top[:, tr % 2], sig[:, tr % 2]).then_inc(top_done, 1)
                if place:
                    v.tensor_tensor_reduce(picked[:, tp % 2, 1], hot[:, tp % 2, 1], spot[:, tp % 2], 1.0, 0.0,
                                           ALU.mult, ALU.add, slotf[:, tp % 2, 1:2]).then_inc(slotf_done, 1)
                if route:
                    dve.wait_ge(top_done, tr + 1)
                    v.max_index(topi[:, tr % 2], top[:, tr % 2], sig[:, tr % 2]).then_inc(topi_done, 1)
                if place:
                    v.tensor_tensor(seen[:, :], seen[:, :], hotb[:, tp % 2], ALU.add).then_inc(seen_done, 1)
                if soft:
                    dve.wait_ge(exp_done, t + 1)
                    v.tensor_reduce(gsum[:, t % 2], prob[:, t % 2], AX.X, ALU.add).then_inc(sum_done, 1)
                if route:
                    dve.wait_ge(topi_done, tr + 1)
                    v.tensor_copy(topf[:, tr % 2], topi[:, tr % 2, 0:2]).then_inc(topf_done, 1)
                if place:
                    dve.wait_ge(slotf_done, 2 * tp + 2)
                    after(dve, scattered[tp % 4], 32 * (tp // 4))
                    v.tensor_copy(slot[:, tp % 4], slotf[:, tp % 2]).then_inc(slot_done, 1)
                if soft:
                    dve.wait_ge(sum_done, t + 1)
                    after(dve, prob_done, t - 1)
                    v.reciprocal(ginv[:, t % 2], gsum[:, t % 2]).then_inc(inv_done, 1)
                if route:
                    dve.wait_ge(topf_done, tr + 1)
                    for r in range(2):
                        v.tensor_scalar(hot[:, tr % 2, r], iota_e[:, :], topf[:, tr % 2, r:r + 1], None,
                                        ALU.is_equal).then_inc(hot_done, 1)
                if work:
                    v_evac(work[0], work[1])
                if route:
                    dve.wait_ge(hot_done, 2 * tr + 2)
                    after(dve, pos_mm, tr - 1)
                    v.tensor_tensor(hotb[:, tr % 2], hot[:, tr % 2, 0], hot[:, tr % 2, 1], ALU.add).then_inc(hotb_done, 1)
                if res1:
                    dve.wait_ge(av_mm, t1_ + 1)
                    dve.wait_ge(ld_xt[t1_ % 4], 16 * (t1_ // 4 + 1))
                    after(dve, t1b_done, t1_ - 1)
                    after(dve, u1_done, t1_ - 1)
                    v.tensor_tensor(t1[:, t1_ % 2], av_p, xt[:, t1_ % 4], ALU.add).then_inc(t1_done, 1)
                    dve.wait_ge(t1_done, t1_ + 1)
                    v.bn_stats(bn1[:, t1_ % 2], t1[:, t1_ % 2]).then_inc(bn1_done, 1)
                    dve.wait_ge(bn1_done, t1_ + 1)
                    after(dve, nmr1_done, t1_ - 1)
                    v.bn_aggr(mv1[:, t1_ % 2], bn1[:, t1_ % 2]).then_inc(mv1_done, 1)
                if work:
                    for c in work[2]:
                        k_evac(work[0], c)

            dve.wait_ge(cnt_mm, 1)
            v.tensor_scalar(blk_i[:, :], cnt_p, 1.0 / BLK, (BLK - 1) / (2 * BLK), ALU.mult, ALU.add).then_inc(plan, 1)
            v.tensor_scalar(tiles_i[:, :], cnt_p, 1.0 / P, (P - 1) / (2 * P), ALU.mult, ALU.add).then_inc(plan, 1)
            v.tensor_tensor(padr[:, :], cnt_p, ebase[:, :], ALU.add).then_inc(plan, 1)
            dve.wait_ge(plan, 3)
            v.tensor_copy(blk_f[:, :], blk_i[:, :]).then_inc(plan, 1)
            v.tensor_copy(tiles_f[:, :], tiles_i[:, :]).then_inc(plan, 1)
            dve.wait_ge(plan, 5)
            v.scalar_tensor_tensor(out=ends[:, 0, :], in0=ebase_b[:, 0, :], scalar=1.0, in1=blk_f[:, :],
                                   op0=ALU.mult, op1=ALU.add).then_inc(plan, 1)
            v.scalar_tensor_tensor(out=ends[:, 1, :], in0=tiles_f[:, :], scalar=float(P // BLK), in1=ebase_b[:, 1, :],
                                   op0=ALU.mult, op1=ALU.add).then_inc(plan, 1)
            v.tensor_tensor(ends[:, 2, :], padr[:, :], eoff_r[:, :], ALU.add).then_inc(plan, 1)
            v.scalar_tensor_tensor(out=ends[:, 3, :], in0=blk_f[:, :], scalar=float(BLK), in1=ebase[:, :],
                                   op0=ALU.mult, op1=ALU.add).then_inc(plan, 1)
            v.tensor_tensor_scan(tincl[:, :], ones_f[:, :], tiles_f[:, :], 0.0, ALU.mult, ALU.add).then_inc(plan, 1)
            dve.wait_ge(plan, 10)
            for n in range(2):
                v.tensor_tensor(tmp_b[:, n], pick_b[:, :, :], ends[:, n, :].unsqueeze(1).to_broadcast([P, PB, NE]),
                                ALU.mult).then_inc(plan, 1)
                v.tensor_tensor(tmp_r[:, n], pick_r[:, :, :], ends[:, 2 + n, :].unsqueeze(1).to_broadcast([P, PR, NE]),
                                ALU.mult).then_inc(plan, 1)
            dve.wait_ge(plan, 14)
            v.tensor_reduce(pad_b[:, :, :], tmp_b[:, :, :, :], AX.X, ALU.add).then_inc(plan, 1)
            v.tensor_reduce(pad_r[:, :, :], tmp_r[:, :, :, :], AX.X, ALU.add).then_inc(plan, 1)
            v.tensor_tensor(texcl[:, :], tincl[:, :], tiles_f[:, :], ALU.subtract).then_inc(plan, 1)
            v.tensor_scalar(at_i[:, :], tincl[:, :], iota_p[:, 0:1], None, ALU.is_le).then_inc(plan, 1)
            dve.wait_ge(plan, 18)
            v.tensor_tensor(pad_b[:, 0, :], pad_b[:, 0, :], off_b[:, :], ALU.add).then_inc(plan, 1)
            v.tensor_tensor(pad_r[:, 0, :], pad_r[:, 0, :], off_r[:, :], ALU.add).then_inc(plan, 1)
            v.tensor_scalar(at_x[:, :], texcl[:, :], iota_p[:, 0:1], None, ALU.is_le).then_inc(plan, 1)
            dve.wait_ge(plan, 21)
            v.tensor_tensor(over_b[:, :], pad_b[:, 0, :], pad_b[:, 1, :], ALU.is_ge).then_inc(plan, 1)
            v.tensor_tensor(over_r[:, :], pad_r[:, 0, :], pad_r[:, 1, :], ALU.is_ge).then_inc(plan, 1)
            v.tensor_tensor(at_x[:, :], at_x[:, :], at_i[:, :], ALU.subtract).then_inc(plan, 1)
            dve.wait_ge(plan, 24)
            v.scalar_tensor_tensor(out=pad_b_i[:, :], in0=over_b[:, :], scalar=float(NE * CAP), in1=pad_b[:, 0, :],
                                   op0=ALU.mult, op1=ALU.add).then_inc(padr_done, 1)
            v.scalar_tensor_tensor(out=pad_r_i[:, :], in0=over_r[:, :], scalar=float(NE * CAP), in1=pad_r[:, 0, :],
                                   op0=ALU.mult, op1=ALU.add).then_inc(padr_done, 1)
            v.scalar_tensor_tensor(out=rowt[:, :], in0=texcl[:, :], scalar=-float(P), in1=ebase[:, :],
                                   op0=ALU.mult, op1=ALU.add).then_inc(plan, 1)
            v.tensor_tensor_reduce(junk[:, 0, :], at_x[:, :], iota_e[:, :], 1.0, 0.0, ALU.mult, ALU.add,
                                   sums[:, 0:1]).then_inc(plan, 1)
            v.tensor_scalar(used[:, :], at_i[:, NE - 1:NE], -1.0, 1.0, ALU.mult, ALU.add).then_inc(plan, 1)
            dve.wait_ge(plan, 27)
            v.tensor_tensor_reduce(junk[:, 1, :], at_x[:, :], rowt[:, :], 1.0, 0.0, ALU.mult, ALU.add,
                                   sums[:, 1:2]).then_inc(plan, 1)
            v.scalar_tensor_tensor(out=sched[:, 0:1], in0=at_i[:, NE - 1:NE], scalar=float(NE - 1), in1=sums[:, 0:1],
                                   op0=ALU.mult, op1=ALU.add).then_inc(sched_done, 1)
            dve.wait_ge(plan, 28)
            v.scalar_tensor_tensor(out=term[:, 0:1], in0=i128[:, :], scalar=used[:, 0:1], in1=sums[:, 1:2],
                                   op0=ALU.mult, op1=ALU.add).then_inc(plan, 1)
            dve.wait_ge(plan, 29)
            v.scalar_tensor_tensor(out=sched[:, 1:2], in0=at_i[:, NE - 1:NE], scalar=float(NE * CAP), in1=term[:, 0:1],
                                   op0=ALU.mult, op1=ALU.add).then_inc(sched_done, 1)
            dve.wait_ge(sched_mm, 1)
            v.tensor_copy(sched_i[:, :, :], sched_p.rearrange("p (a n) -> p a n", a=2)).then_inc(sched_out, 1)

            def hidden(i, g):
                for q in range(2):
                    dve.wait_ge(H_mm, pairs(i, g) + (q + 1))
                    after(dve, HT_mm, pairs(i, g))
                    v.tensor_scalar(hid[:, 2 * q:2 * q + 2, 0:HID], H_p[q], 0.0, None, ALU.max).then_inc(hid_out, 1)

            def columns(i, g):
                dve.wait_ge(ld_rows[g], dma_count(i) + 16 * GROUP)
                after(dve, y_sent[g], dma_count(i))
                v.tensor_copy(dest[:, g, :], xin[:, g, :, ID].bitcast(I32)).then_inc(cols_out, 1)
                v.tensor_copy(wgt[:, g, :], xin[:, g, :, WEIGHT]).then_inc(cols_out, 1)

            def hidden_transposed(i, g):
                for q in range(2):
                    dve.wait_ge(HT_mm, pairs(i, g) + (q + 1))
                    if g >= 2 or not (isinstance(i, int) and i == 0):
                        dve.wait_ge(Y_mm, pairs(i, g) - 2)
                    v.tensor_copy(hT[:, g % 2, 2 * q:2 * q + 2, :], HT_p[q][0:HID]).then_inc(HT_out, 1)

            def weighted(i, g):
                after(dve, y_sent[g], dma_count(i))
                dve.wait_ge(cols_out, pairs(i, g) + 2)
                dve.wait_ge(Y_mm, pairs(i, g) + 2)
                for k in range(2, GROUP):
                    v.tensor_scalar(yb[:, g, k, :], Y_p[1][:, k - 2, :], wgt[:, g, k:k + 1], None, ALU.mult).then_inc(y_out_v, 1)

            def dve_group(i, g, first, last):
                hidden(i, g)
                columns(i, g)
                hidden_transposed(i, g)
                weighted(i, g)

            over_groups(dve, dve_group)

            for c in range(NC_):
                dve.wait_ge(ld_pair[c % 2], 32 * (c // 2 + 1))
                t2c = t2[:, c * CG:(c + 1) * CG, :]
                v.tensor_tensor(t2c, t2c, pair0[:, c % 2], ALU.add).then_inc(half_sum, 1)
                dve.wait_ge(half_sum, c + 1)
                after(dve, stored[c % 2], 16 * (c // 2))
                v.tensor_tensor(fin[:, c % 2], t2c, pair1[:, c % 2], ALU.add).then_inc(out_sum, 1)

        @block.tensor
        def _(pe):
            m = nc.tensor

            def qk_proj(b, c):
                after(pe, v_out, v_evacs[0])
                after(pe, k_out, 2 * b + c)
                after(pe, q_out, 2 * b + c)
                for a in range(CH):
                    mm = m.matmul(bank7[0:2 * QK, :], wqk[:, a, :], xc[:, b % 2, a, c * 512:(c + 1) * 512],
                                  start=(a == 0), stop=(a == CH - 1))
                mm.then_inc(qk_mm, 1)
                qk_evacs[0] += 1

            def v_proj(b, j):
                after(pe, v_out, v_evacs[0])
                after(pe, k_out, qk_evacs[0])
                after(pe, q_out, qk_evacs[0])
                for a in range(CH):
                    mm = m.matmul(bank7[:, 0:C], xc[:, b % 2, a, j * P:(j + 1) * P], wv[:, a, :],
                                  start=(a == 0), stop=(a == CH - 1))
                mm.then_inc(v_mm, 1)
                v_evacs[0] += 1

            v_evacs, qk_evacs = [0], [0]
            pe.wait_ge(ld_wproj, 16 * 5)
            pe.wait_ge(ld_xc[0], 16)
            for c in range(2):
                qk_proj(0, c)
            for j in range(KB):
                v_proj(0, j)
            pe.wait_ge(const_done, 1)
            pe.wait_ge(ld_wmix, 48)

            for s in range(NT + LAST):
                t = s
                if t < NT:
                    b, tb = t // TB, t % TB
                    after(pe, centred, t)
                    pe.wait_ge(q_out, 2 * b + 1 + tb // (TB // 2))
                    pe.wait_ge(k_out, 2 * (b + 1))
                    for w in range(WT):
                        mm = m.matmul(E[:, w * KB * W:(w + 1) * KB * W],
                                      q_s[:, WT * tb + w].rearrange("p g h -> p (g h)"),
                                      k_s[:, b % 2].rearrange("p j v -> p (j v)"), start=True, stop=True)
                    mm.then_inc(e_mm, 1)
                t = s - S_MIX
                if 0 <= t < NT:
                    pe.wait_ge(u1_done, t + 1)
                    after(pe, uh_out, t)
                    tail = t % TB > 0
                    for a in range(CH):
                        cs = slice(a * P, (a + 1) * P)
                        m.transpose(mix_p[:, a, 0, :], u1[:, t % 3, cs], ident[:, :])
                        mm = m.matmul(mix_p[:, a, 1, :], u1[:, t % 3, cs], band[:, 0:P], start=True, stop=not tail)
                        if tail:
                            mm = m.matmul(mix_p[:, a, 1, 0:REACH], u1[P - REACH:P, (t - 1) % 3, cs],
                                          band[P - REACH:P, P:P + REACH], start=False, stop=True)
                    mm.then_inc(mix_mm, 1)
                work = proj_work(s)
                if work:
                    b, j, chunks = work
                    if j == 0:
                        pe.wait_ge(ld_xc[b % 2], 16 * (b // 2 + 1))
                    v_proj(b, j)
                t = s - S_POS
                if 0 <= t:
                    pe.wait_ge(hotb_done, t + 1)
                    after(pe, seen_done, t)
                    after(pe, spot_done, t)
                    pe.wait_ge(ex_done, min(t + 2, NT))
                    m.matmul(pos_p, upper[:, :], hotb[:, t % 2], start=True, stop=False)
                    m.matmul(pos_p, ones_b[:, :], seen[:, :], start=False, stop=True).then_inc(pos_mm, 1)
                t = s - S_AV
                if 0 <= t < NT:
                    b = t // TB
                    pe.wait_ge(prob_done, t + 1)
                    pe.wait_ge(v_out, (b + 1) * KB)
                    after(pe, t1_done, t)
                    pr = prob[:, t % 2].rearrange("p (j w) v -> p j (w v)", w=WT)
                    for j in range(KB):
                        mm = m.matmul(av_p, pr[:, j, :], vT[:, b % 2, j, :], start=(j == 0), stop=(j == KB - 1))
                    mm.then_inc(av_mm, 1)
                t = s - S_NORM2
                if 0 <= t < NT:
                    pe.wait_ge(u2_done, t + 1)
                    after(pe, u2T_out, t)
                    for a in range(CH):
                        mm = m.transpose(t2_p[:, a, :], rows[:, t % 4, 0, a * P:(a + 1) * P], ident[:, :])
                    mm.then_inc(u2T_mm, 1)
                t = s - S_MIX
                if 0 <= t < NT:
                    pe.wait_ge(uh_out, t + 1)
                    after(pe, t2_done, t)
                    for i, (side, a) in enumerate([(0, 0), (0, 1), (1, 0), (1, 1)]):
                        mm = m.matmul(h_p, uh[:, t % 2, a, side, :], (w1s, w2s)[side][:, a, :],
                                      start=(i == 0), stop=(i == 3))
                    mm.then_inc(h_mm, 1)
                t = s - S_NORM2
                if 0 <= t < NT:
                    pe.wait_ge(u2T_out, t + 1)
                    after(pe, ex_done, t)
                    after(pe, spot_done, t - 1)
                    for a in range(CH):
                        mm = m.matmul(lg_p, u2T[:, t % 2, a, :], sels[:, a, :], start=(a == 0), stop=(a == CH - 1))
                    mm.then_inc(lg_mm, 1)
                work = proj_work(s)
                if work:
                    b, j, chunks = work
                    for c in chunks:
                        qk_proj(b, c)

            pe.wait_ge(seen_done, NT)
            m.matmul(cnt_p, ones_b[:, :], seen[:, :], start=True, stop=True).then_inc(cnt_mm, 1)
            pe.wait_ge(sched_done, 2)
            for c in range(2):
                mm = m.matmul(sched_p[:, c * P:(c + 1) * P], sched[:, c:c + 1], ident[:, :], start=True, stop=True)
            mm.then_inc(sched_mm, 1)
            pe.wait_ge(sched_out, 1)
            pe.wait_ge(ld_keys, 32)

            still = hid[:, :, :].rearrange("p k n -> p (k n)").bitcast(BF16)
            for _ in range(WARM):
                m.matmul(bank[7][:, :], ones_b[:, :], still[:, 0:512], start=True, stop=True)

            def transpose_pair(i, g, q):
                if q == 0:
                    pe.wait_ge(ld_rows[g], dma_count(i) + 16 * GROUP)
                    after(pe, T_out, pairs(i, g))
                for k in (2 * q, 2 * q + 1):
                    for a in range(CH):
                        mm = m.transpose(T_p[q][:, k % 2, a, :], xin[:, g, k, a * P:(a + 1) * P], ident[:, :])
                mm.then_inc(T_mm, 1)

            def hidden_pair(i, g, q, expert):
                after(pe, hid_out, pairs(i, g) if q == 0 else 0)
                pe.wait_ge(T_out, pairs(i, g) + (q + 1))
                for k in (2 * q, 2 * q + 1):
                    for a in range(CH):
                        mm = m.matmul(H_p[q][:, k % 2, :], uT[:, k, a, :], keys_s[:, a, bass.ds(expert[k], 1), :],
                                      start=(a == 0), stop=(a == CH - 1))
                mm.then_inc(H_mm, 1)

            def hidden_transpose_pair(i, g, q):
                after(pe, HT_out, pairs(i, g) if q == 0 else 0)
                pe.wait_ge(hid_out, pairs(i, g) + (q + 1))
                for k in (2 * q, 2 * q + 1):
                    mm = m.transpose(HT_p[q][:, k % 2, :], hid[:, k, :], ident[:, :])
                mm.then_inc(HT_mm, 1)

            def output_pair(i, g, q, expert):
                after(pe, (y_out_a, y_out_v)[q], pairs(i, g))
                pe.wait_ge(HT_out, pairs(i, g) + (q + 1))
                for k in (2 * q, 2 * q + 1):
                    mm = m.matmul(Y_p[q][:, k % 2, :], hT[:, g % 2, k, :], values_s[:, bass.ds(expert[k], 1), :],
                                  start=True, stop=True)
                mm.then_inc(Y_mm, 1)

            experts = [pe.alloc_register(f"expert{k}") for k in range(GROUP)]

            def pe_group(i, g, first, last):
                expert = loaded(pe, experts, sched_i[0:1, 0, bass.ds(i * (NB * GROUP) + g * GROUP, GROUP)], NE - 1)
                for q in range(2):
                    hidden_pair(i, g, q, expert)
                for q in range(2):
                    hidden_transpose_pair(i, g, q)
                    if not last:
                        transpose_pair(*following(i, g), q)
                for q in range(2):
                    output_pair(i, g, q, expert)

            for q in range(2):
                transpose_pair(0, 0, q)
            over_groups(pe, pe_group)


def kernel(**inputs):
    import numpy as np
    import concourse.bacc as bacc
    from concourse.bass_utils import run_bass_kernel_spmd

    a = {k: np.asarray(v) for k, v in inputs.items()}
    x = a["x"]
    laid = {
        "x_cm": x.transpose(1, 0, 3, 2).reshape(C, N),
        "x_tok": x.reshape(B, C, HW).transpose(0, 2, 1).reshape(N, C),
        "wqT": a["L0_conv_wq"].T,
        "bq": a["L0_conv_bq"].reshape(QK, 1),
        "wkT": a["L0_conv_wk"].T,
        "bk": a["L0_conv_bk"].reshape(QK, 1),
        "wvT": a["L0_conv_wv"].T,
        "bv": a["L0_conv_bv"].reshape(1, C),
        "gamma": a["L0_conv_gamma"].reshape(1, 1),
        "w1": a["L1_attn_W1"],
        "w2": a["L1_attn_W2"],
        "bias": a["L1_attn_bias"].reshape(1, C),
        "selT": a["L1_ffn_expert_sel"].T,
        "keys": a["L1_ffn_keys"].transpose(1, 0, 2),
        "values": a["L1_ffn_values"].transpose(1, 0, 2),
    }
    laid = {k: np.ascontiguousarray(v) for k, v in laid.items()}

    nc = bacc.Bacc("TRN2", target_bir_lowering=False, num_devices=1)
    args = [nc.dram_tensor(k, v.shape, mybir.dt.from_np(v.dtype), kind="ExternalInput").ap() for k, v in laid.items()]
    args.append(nc.dram_tensor("out", [N, C], F32, kind="ExternalOutput").ap())
    attention_moe(nc, *args)
    r = run_bass_kernel_spmd(nc, [laid], core_ids=[0])
    tokens = r.results[0]["out"]
    return tokens.reshape(B, HW, C).transpose(0, 2, 1).reshape(B, C, H, W)
```

```python
import concourse.bass as bass
from concourse import mybir
from contextlib import ExitStack
import itertools

F32 = mybir.dt.float32
F32R = mybir.dt.float32r
BF16 = mybir.dt.bfloat16
I32 = mybir.dt.int32
U32 = mybir.dt.uint32
ALU = mybir.AluOpType
ACT = mybir.ActivationFunctionType
AX = mybir.AxisListType

P = 128
B, C, H, W = 4, 256, 32, 32
HW = H * W
N = B * HW
TB = HW // P
NT = N // P
CH = C // P
QK = C // 8
WT = P // H
KB = W // WT
REACH = 32
NE, HID = 32, 64
CAP = N + P
ROW = C + 2
ID, WEIGHT = C, C + 1
SLOT_TILES = 2 * N // P + NE
MIN_FULL = (2 * N - NE * (P - 1)) // P
GROUP = 4
NB = 4
BLK = 8
LN_EPS = 1e-5
PB = NE * (P // BLK) // P
PR = NE * BLK // P
FILL_WARM = 6
DRAIN_WARM = 6
PLAN_WARM = 8
FIRST_WARM = 9
WARM = 24
PADROW = 2 * N

S_AV, S_MIX, S_NORM2, S_ROUTE, S_POS = 1, 2, 3, 4, 5
LAST = S_POS


def attention_moe(nc, x_cm, x_tok, wqT, bq, wkT, bk, wvT, bv, gamma, w1, w2, bias, selT, keys, values, out):
    slots_d = nc.dram_tensor("slot_rows", [NE * CAP + P, ROW], F32, kind="Internal").ap()
    pair_d = nc.dram_tensor("expert_outputs", [2 * N, C], F32, kind="Internal").ap()

    with ExitStack() as ctx:
        def sb(name, shape, dt=F32):
            return ctx.enter_context(nc.sbuf_tensor(name, shape, dt))

        def ps(name, shape, dt=F32):
            return ctx.enter_context(nc.psum_tensor(name, shape, dt))

        def sem(name):
            return ctx.enter_context(nc.semaphore(name))

        wqk = sb("wqk", [P, CH, 2 * QK])
        bqk = sb("bqk", [4 * QK, 1])
        wv = sb("wv", [P, CH, C])
        gbv = sb("gbv", [P, C])
        gam = sb("gam", [P, 1])
        w12_hi = sb("w12_hi", [P, 2, CH, C], F32R)
        w12_lo = sb("w12_lo", [P, 2, CH, C], F32R)
        biasb = sb("biasb", [P, C])
        sels = sb("sels", [P, CH, NE])
        keys_s = sb("keys_s", [P, CH, NE, HID])
        values_s = sb("values_s", [HID, NE, C])
        ident = sb("ident", [P, P])
        band = sb("band", [P, P + REACH])
        upper = sb("upper", [P, P], BF16)
        ones_b = sb("ones_b", [P, P], BF16)
        ones_f = sb("ones_f", [P, 2 * NE])
        warm = sb("warm", [P, 512], BF16)
        unused = sb("unused", [P, 1])
        iota_e2 = sb("iota_e2", [P, 2, NE])
        iota_e = iota_e2[:, 0, :]
        lbase = sb("lbase", [P, 2, NE])
        ebase = lbase[:, 0, :]
        iota_p = sb("iota_p", [P, 1])
        out_ids = sb("out_ids", [P, NT, 2], I32)
        pad_rows = sb("pad_rows", [P, BLK, ROW])
        half_neg = sb("half_neg", [P, 1])

        xc_or_xin = sb("xc_or_xin", [P, max(2 * CH * HW, NB * GROUP * ROW)])
        xc = xc_or_xin[:, 0:2 * CH * HW].rearrange("p (b a n) -> p b a n", b=2, a=CH)
        q_s = sb("q_s", [P, W, WT, H])
        wv_hi = sb("wv_hi", [P, CH, C], F32R)
        wv_lo = sb("wv_lo", [P, CH, C], F32R)
        x_hi = sb("x_hi", [P, 2, CH, P], F32R)
        x_lo = sb("x_lo", [P, 2, CH, P], F32R)
        k_s = sb("k_s", [P, 2, KB, W])
        vT = sb("vT", [P, 2, KB, C])
        xt = sb("xt", [P, 4, C])
        prob = sb("prob", [P, 2, KB * WT, W])
        gmax = sb("gmax", [P, 2, WT * KB])
        gsum = sb("gsum", [P, 2, WT * KB])
        ginv = sb("ginv", [P, 2, WT * KB])
        t1 = sb("t1", [P, 2, C])
        t1b = sb("t1b", [P, 2, C])
        bn1 = sb("bn1", [P, 2, 6])
        mv1 = sb("mv1", [P, 2, 2])
        rstd1 = sb("rstd1", [P, 2, 3])
        u1 = sb("u1", [P, 3, C])
        uh_hi = sb("uh_hi", [P, 2, CH, 2, P], F32R)
        uh_lo = sb("uh_lo", [P, 2, CH, 2, P], F32R)
        t2 = sb("t2", [P, NT, C])
        w12 = t2[:, NT - 2 * CH:].rearrange("p (s a) n -> p s a n", s=2)
        bn2 = sb("bn2", [P, 2, 6])
        mv2 = sb("mv2", [P, 2, 2])
        rstd2 = sb("rstd2", [P, 2, 3])
        rows = sb("rows", [P, 4, 2, ROW])
        u2T = sb("u2T", [P, 2, CH, P])
        ex = sb("ex", [P, 2, NE])
        ex1 = sb("ex1", [P, 2, NE])
        sig = sb("sig", [P, 2, NE])
        top = sb("top", [P, 2, 8])
        topi = sb("topi", [P, 2, 8], U32)
        topf = sb("topf", [P, 2, 2])
        hot = sb("hot", [P, 2, 2, NE])
        hotb = sb("hotb", [P, 2, NE], BF16)
        seen = sb("seen", [P, NE], BF16)
        spot = sb("spot", [P, 2, NE])
        picked = sb("picked", [P, 2, 2, NE])
        slotf = sb("slotf", [P, 2, 2])
        slot = sb("slot", [P, 4, 2], I32)

        full_i = sb("full_i", [P, NE], I32)
        lists = sb("lists", [P, 2, NE])
        tiles_i = sb("tiles_i", [P, NE], I32)
        tiles_f = sb("tiles_f", [P, NE])
        tincl, texcl, at_i, at_x = (t1b[:, 0, i * 2 * NE:(i + 1) * 2 * NE] for i in range(4))
        rowt = sb("rowt", [P, 2 * NE])
        padr = sb("padr", [P, NE])
        blk_f = sb("blk_f", [P, NE])
        blk_i = sb("blk_i", [P, NE], I32)
        pick_b = sb("pick_b", [P, PB, NE])
        pick_r = sb("pick_r", [P, PR, NE])
        off_b = sb("off_b", [P, PB])
        off_r = sb("off_r", [P, PR])
        tmp_b = xt[:, 0, 0:2 * PB * NE].rearrange("p (n c e) -> p n c e", n=2, c=PB)
        tmp_r = xt[:, 1, 0:2 * PR * NE].rearrange("p (n c e) -> p n c e", n=2, c=PR)
        ends = xt[:, 2, 0:4 * NE].rearrange("p (n e) -> p n e", n=4)
        ebase_b = sb("ebase_b", [P, 2, NE])
        eoff_r = sb("eoff_r", [P, NE])
        pad_b = sb("pad_b", [P, 2, PB])
        pad_r = sb("pad_r", [P, 2, PR])
        over_b = sb("over_b", [P, PB])
        over_r = sb("over_r", [P, PR])
        pad_b_i = sb("pad_b_i", [P, PB], I32)
        pad_r_i = sb("pad_r_i", [P, PR], I32)
        sched = sb("sched", [P, 2])
        sums = sb("sums", [P, 2])
        i128 = sb("i128", [P, 1])
        used = sb("used", [P, 1])
        term = sb("term", [P, 2])
        junk = xt[:, 3, 0:4 * NE].rearrange("p (n e) -> p n e", n=2)
        sched_i = sb("sched_i", [1, 2, P], I32)

        xin = xc_or_xin[:, 0:NB * GROUP * ROW].rearrange("p (b k r) -> p b k r", b=NB, k=GROUP)
        dest = sb("dest", [P, NB, GROUP], I32)
        wgt = sb("wgt", [P, NB, GROUP])
        uT = prob.rearrange("p b j v -> p b (j v)")[:, 0].rearrange("p (k a n) -> p k a n", k=GROUP, a=CH)
        kk = q_s[:, W // 4:W // 2].rearrange("p w g h -> p (w g h)").rearrange(
            "p (b k a n) -> p b k a n", b=2, k=GROUP, a=CH)
        hT = q_s[0:HID, 0:W // 4].rearrange("p w g h -> p (w g h)").rearrange("p (b k n) -> p b k n", b=2, k=GROUP)
        yb = vT[:, :, :, :].rearrange("p a (b k) n -> p (a b) k n", k=GROUP)

        E = ps("E", [P, WT * KB * W])
        bank = {i: ps(f"bank{i}", [P, 512]) for i in range(2, 8)}
        av_p = bank[2][:, 0:C]
        mix_p = bank[3][:, :].rearrange("p (a s n) -> p a s n", a=CH, s=2)
        h_p = bank[4][:, 0:C]
        t2_p = bank[5][:, 0:C].rearrange("p (a n) -> p a n", a=CH)
        lg_p = bank[6][:, 0:NE]
        pos_p = bank[6][:, NE:2 * NE]
        first_qk_p = [E[:, c * 512:(c + 1) * 512] for c in range(2)]
        v_banks = [2, 3, 4, 5, 6, 7]
        EARLY_V = 5
        cnt_p = bank[3][:, 0:NE]
        sched_p = bank[2][0:1, 0:2 * P]
        T_p = [E[:, q * 512:(q + 1) * 512].rearrange("p (k a n) -> p k a n", k=2, a=CH) for q in range(2)]
        H_p = [bank[2 + q][0:HID, 0:2 * P].rearrange("p (k n) -> p k n", k=2) for q in range(2)]
        Y_p = [bank[6 + q][:, :].rearrange("p (k n) -> p k n", k=2) for q in range(2)]

        ld_wqk, ld_bqk, ld_first = sem("ld_wqk"), sem("ld_bqk"), [sem(f"ld_first{c}") for c in range(2)]
        ld_wv, ld_wmix, ld_bcast, ld_keys = sem("ld_wv"), sem("ld_wmix"), sem("ld_bcast"), sem("ld_keys")
        ld_xc = [sem(f"ld_xc{i}") for i in range(2)]
        ld_xt = [sem(f"ld_xt{i}") for i in range(4)]
        pick_step, q_zero, spare_done, warm_ready = sem("pick_step"), sem("q_zero"), sem("spare_done"), sem("warm_ready")
        const_raw, const_done, gbv_done = sem("const_raw"), sem("const_done"), sem("gbv_done")
        qk_mm, q_out, k_out, v_mm, v_out = sem("qk_mm"), sem("q_out"), sem("k_out"), sem("v_mm"), sem("v_out")
        e_mm, max_done, centred, exp_done = sem("e_mm"), sem("max_done"), sem("centred"), sem("exp_done")
        sum_done, inv_done, prob_done, av_mm = sem("sum_done"), sem("inv_done"), sem("prob_done"), sem("av_mm")
        t1_done, bn1_done, mv1_done, ve1_done = sem("t1_done"), sem("bn1_done"), sem("mv1_done"), sem("ve1_done")
        rstd1_done, u1_done, t1b_done = sem("rstd1_done"), sem("u1_done"), sem("t1b_done")
        wv_hi_done, wv_lo_done = sem("wv_hi_done"), sem("wv_lo_done")
        x_hi_done, x_lo_done = sem("x_hi_done"), sem("x_lo_done")
        w_hi_done, w_lo_done, uh_hi_done = sem("w_hi_done"), sem("w_lo_done"), sem("uh_hi_done")
        mix_mm, uh_out, h_mm, t2_done = sem("mix_mm"), sem("uh_out"), sem("h_mm"), sem("t2_done")
        bn2_done, mv2_done, ve2_done, rstd2_done = sem("bn2_done"), sem("mv2_done"), sem("ve2_done"), sem("rstd2_done")
        u2_done, u2_copied, u2T_mm, u2T_out = sem("u2_done"), sem("u2_copied"), sem("u2T_mm"), sem("u2T_out")
        lg_mm, ex_done, ex1_done, sig_done = sem("lg_mm"), sem("ex_done"), sem("ex1_done"), sem("sig_done")
        top_done, topi_done, topf_done, hot_done = sem("top_done"), sem("topi_done"), sem("topf_done"), sem("hot_done")
        hotb_done, pos_mm, seen_done, spot_done = sem("hotb_done"), sem("pos_mm"), sem("seen_done"), sem("spot_done")
        slotf_done, slot_done, cols_done = sem("slotf_done"), sem("slot_done"), sem("cols_done")
        scattered = [sem(f"scattered{i}") for i in range(4)]
        cnt_mm, plan, padr_done = sem("cnt_mm"), sem("plan"), sem("padr_done")
        sched_done, sched_mm, sched_out = sem("sched_done"), sem("sched_mm"), sem("sched_out")
        ld_rows = [sem(f"ld_rows{i}") for i in range(NB)]
        nmr1_done, nmr2_done, pads_done = sem("nmr1_done"), sem("nmr2_done"), sem("pads_done")
        cols_out, T_mm, T_out, H_mm, hid_out = sem("cols_out"), sem("T_mm"), sem("T_out"), sem("H_mm"), sem("hid_out")
        keys_out, Y_mm, y_out_a, y_out_v = sem("keys_out"), sem("Y_mm"), sem("y_out_a"), sem("y_out_v")
        y_sent = [sem(f"y_sent{i}") for i in range(NB)]
        ld_pair = [sem(f"ld_pair{i}") for i in range(NB * GROUP // 2)]
        half_sum, out_sum = sem("half_sum"), sem("out_sum")
        stored = sem("stored")

        def after(eng, s, n):
            if not isinstance(n, int) or n > 0:
                eng.wait_ge(s, n)

        def computed(eng, value):
            if isinstance(value, int):
                return value
            reg = eng.alloc_register(f"wait_value_{next(number)}")
            eng.reg_mov(reg, value)
            return eng.snap(reg)

        def loaded(eng, regs, words, largest):
            eng.reg_load(regs, words)
            return [eng.snap(r, min_val=0, max_val=largest) for r in regs]

        number = itertools.count()
        ITER = SLOT_TILES // (NB * GROUP)
        FIRST = MIN_FULL // (NB * GROUP)

        def over_groups(eng, step, between=None):
            for i in range(FIRST):
                for g in range(NB):
                    step(i, g, i == 0 and g == 0, False)
            if between:
                between()
            with eng.Fori(FIRST, ITER - 1) as i:
                for g in range(NB):
                    step(i, g, False, False)
            for g in range(NB):
                step(ITER - 1, g, False, g == NB - 1)

        def following(i, g):
            return (i, g + 1) if g < NB - 1 else (i + 1, 0)

        def pairs(i, g):
            return i * (2 * NB) + 2 * g

        def groups(i, g):
            return i * NB + g

        def dma_count(i):
            return i * (16 * GROUP)
        CG = 2
        CHUNKS = NT // CG
        DEPTH = NB * GROUP // CG
        pair_buf = [yb.rearrange("p b k n -> p (b k) n").rearrange("p (d t) n -> p d t n", t=CG),
                    xc_or_xin[:, 0:NB * GROUP * C].rearrange("p (d t n) -> p d t n", t=CG, n=C)]

        def proj_work(s):
            b, j = s // TB + 1, s % TB
            if b >= B:
                return None
            return b, j, ([j - (TB - 2)] if j >= TB - 2 else [])

        def qk_bank(b, c):
            return first_qk_p[c] if b == 0 else bank[7]

        def v_bank(b, j):
            if b == 0:
                return bank[v_banks[j % len(v_banks)]]
            return bank[5][:, C:2 * C] if j >= TB - 2 else bank[7]

        def xc_loads(b):
            return 16 * (b // 2 + b % 2)

        def v_no(b, j):
            return b * KB + j

        def x_part(n):
            b, j = n // KB + 1, n % KB
            return xc[:, b % 2, :, j * P:(j + 1) * P]

        def wait_x_part(eng, n):
            b, j = n // KB + 1, n % KB
            if j == 0:
                eng.wait_ge(ld_xc[b % 2], xc_loads(b))
            if n >= 2:
                eng.wait_ge(v_mm, v_no(b, j) - 1)

        SPLITS = (B - 1) * KB

        block = ctx.enter_context(nc.Block())

        @block.sync
        def _(sp):
            half = "(a p) n -> p a n"
            sp.dma_start(wqk[:, :, 0:QK], wqT.rearrange(half, p=P)).then_inc(ld_wqk, 16)
            sp.dma_start(wqk[:, :, QK:2 * QK], wkT.rearrange(half, p=P)).then_inc(ld_wqk, 16)
            for c in range(2):
                sp.dma_start(xc[:, 0, :, c * HW // 2:(c + 1) * HW // 2],
                             x_cm[:, c * HW // 2:(c + 1) * HW // 2].rearrange(half, p=P)).then_inc(ld_first[c], 16)
            for r in range(2):
                sp.dma_start(bqk[2 * r * QK:(2 * r + 1) * QK, :], bq).then_inc(ld_bqk, 16)
                sp.dma_start(bqk[(2 * r + 1) * QK:2 * (r + 1) * QK, :], bk).then_inc(ld_bqk, 16)
            sp.dma_start(wv[:, :, :], wvT.rearrange(half, p=P)).then_inc(ld_wv, 16)
            sp.dma_start(gbv[:, :], bv.to_broadcast([P, C])).then_inc(ld_bcast, 16)
            sp.dma_start(gam[:, :], gamma.to_broadcast([P, 1])).then_inc(ld_bcast, 16)
            sp.dma_start(biasb[:, :], bias.to_broadcast([P, C])).then_inc(ld_bcast, 16)
            sp.dma_start(xc[:, 1, :, :], x_cm[:, HW:2 * HW].rearrange(half, p=P)).then_inc(ld_xc[1], 16)
            sp.dma_start(w12[:, 0], w1.rearrange(half, p=P)).then_inc(ld_wmix, 16)
            sp.dma_start(w12[:, 1], w2.rearrange(half, p=P)).then_inc(ld_wmix, 16)
            sp.dma_start(sels[:, :, :], selT.rearrange(half, p=P)).then_inc(ld_wmix, 16)
            for t in range(NT):
                if t == 4:
                    sp.dma_start(keys_s[:, :, :, :], keys.rearrange("(a p) e h -> p a e h", p=P)).then_inc(ld_keys, 16)
                    sp.dma_start(values_s[:, :, :], values).then_inc(ld_keys, 16)
                if t >= 4:
                    sp.wait_ge(t1_done, t - 3)
                sp.dma_start(xt[:, t % 4, :], x_tok[t * P:(t + 1) * P, :]).then_inc(ld_xt[t % 4], 16)
                b = t // TB + 2
                if t % TB == 4 and 2 <= b < B:
                    sp.wait_ge(v_mm, v_no(b - 2, KB - 1) + 1)
                    sp.wait_ge(qk_mm, 4 * (b - 1))
                    sp.dma_start(xc[:, b % 2, :, :],
                                 x_cm[:, b * HW:(b + 1) * HW].rearrange(half, p=P)).then_inc(ld_xc[b % 2], 16)

            sp.wait_ge(const_done, 1)
            sp.dma_start(slots_d[NE * CAP:NE * CAP + P, :], pad_rows[:, 0, :]).then_inc(spare_done, 16)
            sp.wait_ge(spare_done, 16)
            for i in range(4):
                sp.wait_ge(scattered[i], 2 * 16 * (NT // 4))
            sp.wait_ge(sched_out, 1)

            starts = [sp.alloc_register(f"start{k}") for k in range(GROUP)]

            def load_group(i, g, first, last):
                start = loaded(sp, starts, sched_i[0:1, 1, bass.ds(i * (NB * GROUP) + g * GROUP, GROUP)], NE * CAP)
                done = computed(sp, pairs(i, g) - 2 * NB + 2)
                sp.wait_ge(sched_out, 1)
                if not (isinstance(i, int) and i == 0):
                    sp.wait_ge(T_mm, done)
                    sp.wait_ge(cols_out, done)
                for k in range(GROUP):
                    sp.dma_start(xin[:, g, k, :], slots_d[bass.ds(start[k], P), :]).then_inc(ld_rows[g], 16)

            over_groups(sp, load_group, between=lambda: sp.wait_ge(pads_done, 16 * (PB + PR)))

            for g in range(NB):
                sp.wait_ge(y_sent[g], 16 * SLOT_TILES // NB)
            for c in range(CHUNKS):
                if c >= DEPTH:
                    sp.wait_ge(out_sum, c - DEPTH + 1)
                for r in range(2):
                    src = pair_d[r * N + c * CG * P:r * N + (c + 1) * CG * P, :]
                    sp.dma_start(pair_buf[r][:, c % DEPTH], src.rearrange("(t p) n -> p t n", p=P)).then_inc(
                        ld_pair[c % DEPTH], 16)

        @block.gpsimd
        def _(pool):
            g = nc.gpsimd
            g.memset(q_s[:, :, :, :], 0.0).then_inc(q_zero, 1)
            g.memset(ident[:, :], 0.0).then_inc(const_raw, 1)
            g.memset(upper[:, :], 1.0).then_inc(const_raw, 1)
            g.iota(band[:, :], pattern=[[1, P + REACH]], base=0, channel_multiplier=-1,
                   allow_small_or_imprecise_dtypes=True).then_inc(const_raw, 1)
            g.memset(pad_rows[:, :, :], 0.0).then_inc(const_raw, 1)
            g.memset(half_neg[:, :], -0.5)
            g.memset(ones_b[:, :], 1.0)
            g.memset(ones_f[:, :], 1.0)
            g.memset(seen[:, :], 0.0)
            g.iota(iota_e2[:, :, :], pattern=[[0, 2], [1, NE]], base=0, channel_multiplier=0, allow_small_or_imprecise_dtypes=True)
            g.iota(ebase[:, :], pattern=[[CAP, NE]], base=0, channel_multiplier=0, allow_small_or_imprecise_dtypes=True)
            g.iota(iota_p[:, :], pattern=[[0, 1]], base=0, channel_multiplier=1, allow_small_or_imprecise_dtypes=True)
            g.iota(i128[:, :], pattern=[[0, 1]], base=0, channel_multiplier=P, allow_small_or_imprecise_dtypes=True)
            for cols, pick, per in ((PB, pick_b, P // BLK), (PR, pick_r, BLK)):
                g.memset(pick[:, :, :], 1.0).then_inc(pick_step, 1)
            for n, (cols, pick, per) in enumerate(((PB, pick_b, P // BLK), (PR, pick_r, BLK))):
                pool.wait_ge(pick_step, 2 + 2 * n)
                g.affine_select(out=pick[:, :, :], in_=pick[:, :, :], compare_op=ALU.is_ge, fill=0.0, base=0,
                                pattern=[[P, cols], [-per, NE]], channel_multiplier=1).then_inc(pick_step, 1)
                pool.wait_ge(pick_step, 3 + 2 * n)
                g.affine_select(out=pick[:, :, :], in_=pick[:, :, :], compare_op=ALU.is_ge, fill=0.0, base=per - 1,
                                pattern=[[-P, cols], [per, NE]], channel_multiplier=-1).then_inc(pick_step, 1)
            g.iota(ebase_b[:, 0, :], pattern=[[CAP // BLK - P // BLK, NE]], base=0, channel_multiplier=0,
                   allow_small_or_imprecise_dtypes=True)
            g.iota(ebase_b[:, 1, :], pattern=[[CAP // BLK, NE]], base=0, channel_multiplier=0,
                   allow_small_or_imprecise_dtypes=True)
            g.iota(eoff_r[:, :], pattern=[[-BLK, NE]], base=0, channel_multiplier=0, allow_small_or_imprecise_dtypes=True)
            g.iota(off_b[:, :], pattern=[[P, PB]], base=0, channel_multiplier=1, allow_small_or_imprecise_dtypes=True)
            g.iota(off_r[:, :], pattern=[[P, PR]], base=0, channel_multiplier=1, allow_small_or_imprecise_dtypes=True)
            g.iota(out_ids[:, :, :], pattern=[[P, NT], [N, 2]], base=0, channel_multiplier=1).then_inc(const_raw, 1)
            pool.wait_ge(const_raw, 5)
            g.affine_select(out=ident[:, :], in_=ident[:, :], compare_op=ALU.not_equal, fill=1.0, base=0,
                            pattern=[[-1, P]], channel_multiplier=1).then_inc(const_raw, 1)
            g.affine_select(out=upper[:, :], in_=upper[:, :], compare_op=ALU.is_gt, fill=0.0, base=0,
                            pattern=[[1, P]], channel_multiplier=-1).then_inc(const_raw, 1)
            g.affine_select(out=band[:, :], in_=band[:, :], compare_op=ALU.is_gt, fill=0.0, base=0,
                            pattern=[[1, P + REACH]], channel_multiplier=-1).then_inc(const_raw, 1)
            g.iota(pad_rows[:, :, ID].bitcast(I32), pattern=[[1, BLK]], base=PADROW,
                   channel_multiplier=BLK).then_inc(const_raw, 1)
            pool.wait_ge(const_raw, 9)
            g.affine_select(out=band[:, :], in_=band[:, :], compare_op=ALU.is_ge, fill=0.0, base=REACH,
                            pattern=[[-1, P + REACH]], channel_multiplier=1).then_inc(const_done, 1)

            def layer_norm_factors(t, mv, mv_done, rstd, used, ve_done, rstd_done, nmr_done):
                pool.wait_ge(mv_done, t + 1)
                after(pool, used, t - 1)
                g.tensor_scalar(rstd[:, t % 2, 0:1], mv[:, t % 2, 1:2], LN_EPS, None, ALU.add).then_inc(ve_done, 1)
                pool.wait_ge(ve_done, t + 1)
                g.tensor_tensor(rstd[:, t % 2, 1:2], rstd[:, t % 2, 0:1], half_neg[:, :], ALU.pow).then_inc(rstd_done, 1)
                pool.wait_ge(rstd_done, t + 1)
                g.tensor_scalar(rstd[:, t % 2, 2:3], mv[:, t % 2, 0:1], rstd[:, t % 2, 1:2], -1.0,
                                ALU.mult, ALU.mult).then_inc(nmr_done, 1)

            def scatter_rows(t, r):
                g.indirect_dma_start(
                    out=slots_d, out_offset=bass.IndirectOffsetOnAxis(ap=slot[:, t % 4, r:r + 1], axis=0),
                    in_=rows[:, t % 4, r, :], in_offset=None).then_inc(scattered[t % 4], 16)

            def x_low(n):
                wait_x_part(pool, n)
                pool.wait_ge(x_hi_done, n + 1)
                g.tensor_tensor(x_lo[:, n % 2], x_part(n), x_hi[:, n % 2].bitcast(F32), ALU.subtract).then_inc(x_lo_done, 1)

            pool.wait_ge(wv_hi_done, 1)
            g.tensor_tensor(wv_lo[:, :, :], wv[:, :, :], wv_hi[:, :, :].bitcast(F32), ALU.subtract).then_inc(wv_lo_done, 1)
            x_low(0)
            pool.wait_ge(w_hi_done, 1)
            g.tensor_tensor(w12_lo[:, :, :, :], w12[:, :, :, :], w12_hi[:, :, :, :].bitcast(F32),
                            ALU.subtract).then_inc(w_lo_done, 1)
            for s in range(NT + LAST + 1):
                sent = s - 1 - S_POS
                if 0 <= sent:
                    pool.wait_ge(cols_done, 2 * sent + 2)
                    scatter_rows(sent, 0)
                t = s - S_NORM2
                if 0 <= t < NT:
                    layer_norm_factors(t, mv2, mv2_done, rstd2, u2_copied, ve2_done, rstd2_done, nmr2_done)
                if 0 <= sent:
                    scatter_rows(sent, 1)
                t = s - S_MIX
                if 0 <= t < NT:
                    after(pool, t2_done, t - 1)
                    if t == 0:
                        pool.wait_ge(ld_bcast, 48)
                    g.tensor_tensor(t1b[:, t % 2], t1[:, t % 2], biasb[:, :], ALU.add).then_inc(t1b_done, 1)
                if s + 1 < SPLITS:
                    x_low(s + 1)
                t = s - S_AV
                if 0 <= t < NT:
                    layer_norm_factors(t, mv1, mv1_done, rstd1, u1_done, ve1_done, rstd1_done, nmr1_done)
                t = s
                if t < NT:
                    pool.wait_ge(inv_done, t + 1)
                    g.tensor_tensor(prob[:, t % 2], prob[:, t % 2],
                                    ginv[:, t % 2].unsqueeze(2).to_broadcast([P, WT * KB, W]),
                                    ALU.mult).then_inc(prob_done, 1)
                t = s - S_POS
                if 0 <= t < NT:
                    pool.wait_ge(slot_done, t + 1)
                    pool.wait_ge(u2_copied, t + 1)
                    g.tensor_copy(rows[:, t % 4, :, ID].bitcast(I32), out_ids[:, t, :]).then_inc(cols_done, 1)
                    g.tensor_copy(rows[:, t % 4, :, WEIGHT], top[:, t % 2, 0:2]).then_inc(cols_done, 1)

            pool.wait_ge(padr_done, 2)
            blocks_d = slots_d.rearrange("(n k) c -> n (k c)", k=BLK)

            def fill_block(c):
                g.indirect_dma_start(
                    out=blocks_d, out_offset=bass.IndirectOffsetOnAxis(ap=pad_b_i[:, c:c + 1], axis=0),
                    in_=pad_rows[:, :, :].rearrange("p k c -> p (k c)"), in_offset=None,
                    bounds_check=NE * CAP // BLK - 1, oob_is_err=False).then_inc(pads_done, 16)

            def fill_row(c):
                g.indirect_dma_start(
                    out=slots_d, out_offset=bass.IndirectOffsetOnAxis(ap=pad_r_i[:, c:c + 1], axis=0),
                    in_=pad_rows[:, 0, :], in_offset=None,
                    bounds_check=NE * CAP - 1, oob_is_err=False).then_inc(pads_done, 16)

            for c in range(PR):
                fill_row(c)

            def send_group(i, gr):
                copied = computed(pool, pairs(i, gr) + 2)
                for k in range(GROUP):
                    weighted = computed(pool, pairs(i, gr) + (k % 2 + 1))
                    pool.wait_ge(sched_out, 1)
                    pool.wait_ge(cols_out, copied)
                    pool.wait_ge(y_out_a if k < 2 else y_out_v, weighted)
                    g.indirect_dma_start(
                        out=pair_d, out_offset=bass.IndirectOffsetOnAxis(ap=dest[:, gr, k:k + 1], axis=0),
                        in_=yb[:, gr, k, :], in_offset=None,
                        bounds_check=2 * N - 1, oob_is_err=False).then_inc(y_sent[gr], 16)

            def pool_group(i, gr, first, last):
                send_group(i, gr)
                if isinstance(i, int) and i == 0:
                    for c in range(PB)[2 * gr:2 * gr + 2]:
                        fill_block(c)

            assert PB <= 2 * NB
            over_groups(pool, pool_group)

        @block.scalar
        def _(act):
            a = nc.scalar

            def q_evac(b, c):
                act.wait_ge(qk_mm, 2 * (2 * b + c + 1))
                after(act, e_mm, TB * (b - 1) + (c + 1) * TB // 2)
                if b == 0:
                    act.wait_ge(q_zero, 1)
                for r in range(2):
                    w0, rows_r = c * W // 2 + r * W // 4, slice(r * 2 * QK, r * 2 * QK + QK)
                    for g in range(WT):
                        qa = a.activation(q_s[g * QK:(g + 1) * QK, w0:w0 + W // 4, g, :],
                                          qk_bank(b, c)[rows_r, 0:256].rearrange("p (w h) -> p w h", h=H),
                                          ACT.Identity, bias=bqk[rows_r, 0:1])
                qa.then_inc(q_out, 1)

            def x_high(n):
                wait_x_part(act, n)
                a.activation(x_hi[:, n % 2], x_part(n), ACT.Copy).then_inc(x_hi_done, 1)

            act.wait_ge(warm_ready, 1)
            a.activation(unused[:, :], warm[:, 0:1], ACT.Identity)
            act.wait_ge(ld_bqk, 16 * 4)
            for c in range(2):
                q_evac(0, c)
            act.wait_ge(ld_wv, 16)
            a.activation(wv_hi[:, :, :], wv[:, :, :], ACT.Copy).then_inc(wv_hi_done, 1)
            x_high(0)
            act.wait_ge(ld_wmix, 48)
            a.activation(w12_hi[:, :, :, :], w12[:, :, :, :], ACT.Copy).then_inc(w_hi_done, 1)
            for s in range(NT + LAST):
                t = s - S_MIX
                if 0 <= t < NT:
                    act.wait_ge(mix_mm, t + 1)
                    after(act, h_mm, t - 1)
                    a.activation(uh_hi[:, t % 2], mix_p, ACT.Copy).then_inc(uh_hi_done, 1)
                t = s
                if t < NT:
                    act.wait_ge(centred, t + 1)
                    a.activation(prob[:, t % 2], prob[:, t % 2], ACT.Exp).then_inc(exp_done, 1)
                t = s - S_NORM2
                if 0 <= t < NT:
                    act.wait_ge(nmr2_done, t + 1)
                    after(act, scattered[t % 4], 32 * (t // 4))
                    for r, done in enumerate((u2_done, u2_copied)):
                        a.activation(rows[:, t % 4, r, 0:C], t2[:, t], ACT.Identity, bias=rstd2[:, t % 2, 2:3],
                                     scale=rstd2[:, t % 2, 1:2]).then_inc(done, 1)
                if s + 1 < SPLITS:
                    x_high(s + 1)
                if 0 <= t < NT:
                    act.wait_ge(u2T_mm, t + 1)
                    after(act, lg_mm, t - 1)
                    a.activation(u2T[:, t % 2], t2_p, ACT.Copy).then_inc(u2T_out, 1)
                t = s - S_NORM2
                if 0 <= t < NT:
                    act.wait_ge(lg_mm, t + 1)
                    after(act, ex1_done, t - 1)
                    a.activation(ex[:, t % 2], lg_p, ACT.Exp, scale=-1.0).then_inc(ex_done, 1)
                t = s - S_AV
                if 0 <= t < NT:
                    act.wait_ge(nmr1_done, t + 1)
                    after(act, mix_mm, t - 1)
                    a.activation(u1[:, t % 3], t1[:, t % 2], ACT.Identity, bias=rstd1[:, t % 2, 2:3],
                                 scale=rstd1[:, t % 2, 1:2]).then_inc(u1_done, 1)
                work = proj_work(s)
                if work:
                    for c in work[2]:
                        q_evac(work[0], c)

            def transposed(i, g):
                for q in range(2):
                    act.wait_ge(T_mm, pairs(i, g) + (q + 1))
                    after(act, H_mm, pairs(i, g))
                    a.activation(uT[:, 2 * q:2 * q + 2], T_p[q], ACT.Copy).then_inc(T_out, 1)

            def weighted(i, g):
                after(act, y_sent[g], dma_count(i))
                act.wait_ge(cols_out, pairs(i, g) + 2)
                act.wait_ge(Y_mm, pairs(i, g) + 1)
                for k in range(2):
                    a.activation(yb[:, g, k, :], Y_p[0][:, k, :], ACT.Copy, scale=wgt[:, g, k:k + 1]).then_inc(y_out_a, 1)

            experts = [act.alloc_register(f"keys_expert{k}") for k in range(GROUP)]

            def keys_copied(i, g):
                expert = loaded(act, experts, sched_i[0:1, 0, bass.ds(i * (NB * GROUP) + g * GROUP, GROUP)], NE - 1)
                after(act, H_mm, pairs(i, g) - 2 if g >= 2 or not (isinstance(i, int) and i == 0) else 0)
                for k in range(GROUP):
                    done = a.activation(kk[:, g % 2, k], keys_s[:, :, bass.ds(expert[k], 1), :].rearrange(
                        "p a e n -> p a (e n)"), ACT.Copy)
                done.then_inc(keys_out, 1)

            def act_group(i, g, first, last):
                if not last:
                    keys_copied(*following(i, g))
                    transposed(*following(i, g))
                weighted(i, g)

            act.wait_ge(sched_out, 1)
            act.wait_ge(ld_keys, 32)
            keys_copied(0, 0)
            transposed(0, 0)
            over_groups(act, act_group)

            for c in range(CHUNKS):
                act.wait_ge(out_sum, c + 1)
                rows_out = out[c * CG * P:(c + 1) * CG * P, :].rearrange("(t p) n -> p t n", p=P)
                act.dma_start(rows_out, t2[:, c * CG:(c + 1) * CG]).then_inc(stored, 16)
            act.wait_ge(stored, 16 * CHUNKS)

        @block.vector
        def _(dve):
            v = nc.vector

            def k_evac(b, c):
                dve.wait_ge(qk_mm, 2 * (2 * b + c + 1))
                after(dve, e_mm, TB * (b - 1))
                for r in range(2):
                    v0, rows_r = c * W // 2 + r * W // 4, slice(r * 2 * QK + QK, (r + 1) * 2 * QK)
                    for g in range(WT):
                        src = qk_bank(b, c)[rows_r, 0:256].rearrange("p (v j g) -> p g j v", g=WT, j=KB)[:, g]
                        ka = v.tensor_scalar(k_s[g * QK:(g + 1) * QK, b % 2, :, v0:v0 + W // 4], src,
                                             bqk[rows_r, 0:1], None, ALU.add)
                ka.then_inc(k_out, 1)

            def v_evac(b, j):
                dve.wait_ge(v_mm, v_no(b, j) + 1)
                after(dve, av_mm, TB * (b - 1))
                v.scalar_tensor_tensor(out=vT[:, b % 2, j, :], in0=v_bank(b, j)[:, 0:C], scalar=gam[:, 0:1], in1=gbv[:, :],
                                       op0=ALU.mult, op1=ALU.add).then_inc(v_out, 1)

            v.memset(warm[:, :], 0.0).then_inc(warm_ready, 1)
            dve.wait_ge(ld_bcast, 48)
            v.tensor_scalar(gbv[:, :], gbv[:, :], gam[:, 0:1], None, ALU.mult).then_inc(gbv_done, 1)
            dve.wait_ge(ld_bqk, 16 * 4)
            for c in range(2):
                k_evac(0, c)
            dve.wait_ge(gbv_done, 1)
            for j in range(EARLY_V):
                v_evac(0, j)

            for s in range(NT + LAST):
                t, t1_, tm, t2_, tr, tp = s, s - S_AV, s - S_MIX, s - S_NORM2, s - S_ROUTE, s - S_POS
                soft, res1, res2 = t < NT, 0 <= t1_ < NT, 0 <= t2_ < NT
                route, place = 0 <= tr < NT, 0 <= tp < NT
                work = proj_work(s)
                if res2:
                    dve.wait_ge(h_mm, t2_ + 1)
                    dve.wait_ge(t1b_done, t2_ + 1)
                    v.tensor_tensor(t2[:, t2_], h_p, t1b[:, t2_ % 2], ALU.add).then_inc(t2_done, 1)
                if soft:
                    dve.wait_ge(e_mm, t + 1)
                    v.tensor_reduce(gmax[:, t % 2], E[:, :].rearrange("p (a v) -> p a v", v=W),
                                    AX.X, ALU.max).then_inc(max_done, 1)
                if res2:
                    dve.wait_ge(t2_done, t2_ + 1)
                    v.bn_stats(bn2[:, t2_ % 2], t2[:, t2_]).then_inc(bn2_done, 1)
                if soft:
                    dve.wait_ge(max_done, t + 1)
                    after(dve, av_mm, t - 1)
                    v.tensor_tensor(prob[:, t % 2].rearrange("p (j w) v -> p w j v", w=WT),
                                    E[:, :].rearrange("p (w j v) -> p w j v", w=WT, v=W),
                                    gmax[:, t % 2].rearrange("p (w j) -> p w j", w=WT).unsqueeze(3)
                                    .to_broadcast([P, WT, KB, W]), ALU.subtract).then_inc(centred, 1)
                if s == 0:
                    for j in range(EARLY_V, KB):
                        v_evac(0, j)
                    dve.wait_ge(const_done, 1)
                if res2:
                    dve.wait_ge(bn2_done, t2_ + 1)
                    after(dve, nmr2_done, t2_ - 1)
                    v.bn_aggr(mv2[:, t2_ % 2], bn2[:, t2_ % 2]).then_inc(mv2_done, 1)
                if route:
                    dve.wait_ge(ex_done, tr + 1)
                    v.tensor_scalar(ex1[:, tr % 2], ex[:, tr % 2], 1.0, None, ALU.add).then_inc(ex1_done, 1)
                if place:
                    dve.wait_ge(pos_mm, tp + 1)
                    v.tensor_tensor(spot[:, tp % 2], pos_p, ebase[:, :], ALU.add).then_inc(spot_done, 1)
                if route:
                    dve.wait_ge(ex1_done, tr + 1)
                    v.reciprocal(sig[:, tr % 2], ex1[:, tr % 2]).then_inc(sig_done, 1)
                if place:
                    dve.wait_ge(spot_done, tp + 1)
                    v.tensor_tensor_reduce(picked[:, tp % 2, 0], hot[:, tp % 2, 0], spot[:, tp % 2], 1.0, 0.0,
                                           ALU.mult, ALU.add, slotf[:, tp % 2, 0:1]).then_inc(slotf_done, 1)
                if route:
                    dve.wait_ge(sig_done, tr + 1)
                    after(dve, cols_done, 2 * (tr - 1))
                    v.max(top[:, tr % 2], sig[:, tr % 2]).then_inc(top_done, 1)
                if place:
                    v.tensor_tensor_reduce(picked[:, tp % 2, 1], hot[:, tp % 2, 1], spot[:, tp % 2], 1.0, 0.0,
                                           ALU.mult, ALU.add, slotf[:, tp % 2, 1:2]).then_inc(slotf_done, 1)
                if route:
                    dve.wait_ge(top_done, tr + 1)
                    v.max_index(topi[:, tr % 2], top[:, tr % 2], sig[:, tr % 2]).then_inc(topi_done, 1)
                if place and tp < NT - 1:
                    v.tensor_tensor(seen[:, :], seen[:, :], hotb[:, tp % 2], ALU.add).then_inc(seen_done, 1)
                if 0 <= tm < NT:
                    dve.wait_ge(uh_hi_done, tm + 1)
                    v.tensor_tensor(uh_lo[:, tm % 2], mix_p, uh_hi[:, tm % 2].bitcast(F32), ALU.subtract).then_inc(uh_out, 1)
                if soft:
                    dve.wait_ge(exp_done, t + 1)
                    v.tensor_reduce(gsum[:, t % 2], prob[:, t % 2], AX.X, ALU.add).then_inc(sum_done, 1)
                if route:
                    dve.wait_ge(topi_done, tr + 1)
                    v.tensor_copy(topf[:, tr % 2], topi[:, tr % 2, 0:2]).then_inc(topf_done, 1)
                if place:
                    dve.wait_ge(slotf_done, 2 * tp + 2)
                    after(dve, scattered[tp % 4], 32 * (tp // 4))
                    v.tensor_copy(slot[:, tp % 4], slotf[:, tp % 2]).then_inc(slot_done, 1)
                if soft:
                    dve.wait_ge(sum_done, t + 1)
                    after(dve, prob_done, t - 1)
                    v.reciprocal(ginv[:, t % 2], gsum[:, t % 2]).then_inc(inv_done, 1)
                if res1:
                    dve.wait_ge(av_mm, t1_ + 1)
                    dve.wait_ge(ld_xt[t1_ % 4], 16 * (t1_ // 4 + 1))
                    after(dve, t1b_done, t1_ - 1)
                    after(dve, u1_done, t1_ - 1)
                    v.tensor_tensor(t1[:, t1_ % 2], av_p, xt[:, t1_ % 4], ALU.add).then_inc(t1_done, 1)
                if route:
                    dve.wait_ge(topf_done, tr + 1)
                    for r in range(2):
                        v.tensor_scalar(hot[:, tr % 2, r], iota_e[:, :], topf[:, tr % 2, r:r + 1], None,
                                        ALU.is_equal).then_inc(hot_done, 1)
                if res1:
                    dve.wait_ge(t1_done, t1_ + 1)
                    v.bn_stats(bn1[:, t1_ % 2], t1[:, t1_ % 2]).then_inc(bn1_done, 1)
                if route:
                    dve.wait_ge(hot_done, 2 * tr + 2)
                    after(dve, pos_mm, tr - 1)
                    v.tensor_tensor(hotb[:, tr % 2], hot[:, tr % 2, 0], hot[:, tr % 2, 1], ALU.add).then_inc(hotb_done, 1)
                if res1:
                    dve.wait_ge(bn1_done, t1_ + 1)
                    after(dve, nmr1_done, t1_ - 1)
                    v.bn_aggr(mv1[:, t1_ % 2], bn1[:, t1_ % 2]).then_inc(mv1_done, 1)
                if work and not work[2]:
                    v_evac(work[0], work[1])
                if work and work[2]:
                    for c in work[2]:
                        k_evac(work[0], c)
                    v_evac(work[0], work[1])

            dve.wait_ge(cnt_mm, 1)
            v.tensor_scalar(full_i[:, :], cnt_p, 1.0 / P, -(P - 1) / (2 * P), ALU.mult, ALU.add).then_inc(plan, 1)
            v.tensor_scalar(tiles_i[:, :], cnt_p, 1.0 / P, (P - 1) / (2 * P), ALU.mult, ALU.add).then_inc(plan, 1)
            v.tensor_scalar(blk_i[:, :], cnt_p, 1.0 / BLK, (BLK - 1) / (2 * BLK), ALU.mult, ALU.add).then_inc(plan, 1)
            v.tensor_tensor(padr[:, :], cnt_p, ebase[:, :], ALU.add).then_inc(plan, 1)
            dve.wait_ge(plan, 4)
            v.tensor_copy(lists[:, 0, :], full_i[:, :]).then_inc(plan, 1)
            v.tensor_copy(tiles_f[:, :], tiles_i[:, :]).then_inc(plan, 1)
            v.tensor_copy(blk_f[:, :], blk_i[:, :]).then_inc(plan, 1)
            dve.wait_ge(plan, 7)
            v.tensor_tensor(lists[:, 1, :], tiles_f[:, :], lists[:, 0, :], ALU.subtract).then_inc(plan, 1)
            v.scalar_tensor_tensor(out=lbase[:, 1, :], in0=lists[:, 0, :], scalar=float(P), in1=ebase[:, :],
                                   op0=ALU.mult, op1=ALU.add).then_inc(plan, 1)
            dve.wait_ge(plan, 9)
            v.tensor_tensor_scan(tincl[:, :], ones_f[:, :], lists[:, :, :].rearrange("p a e -> p (a e)"), 0.0,
                                 ALU.mult, ALU.add).then_inc(plan, 1)
            dve.wait_ge(plan, 10)
            v.tensor_tensor(texcl[:, :], tincl[:, :], lists[:, :, :].rearrange("p a e -> p (a e)"),
                            ALU.subtract).then_inc(plan, 1)
            v.tensor_scalar(at_i[:, :], tincl[:, :], iota_p[:, 0:1], None, ALU.is_le).then_inc(plan, 1)
            dve.wait_ge(plan, 12)
            v.tensor_scalar(at_x[:, :], texcl[:, :], iota_p[:, 0:1], None, ALU.is_le).then_inc(plan, 1)
            v.scalar_tensor_tensor(out=rowt[:, :], in0=texcl[:, :], scalar=-float(P),
                                   in1=lbase[:, :, :].rearrange("p a e -> p (a e)"),
                                   op0=ALU.mult, op1=ALU.add).then_inc(plan, 1)
            v.tensor_scalar(used[:, :], at_i[:, 2 * NE - 1:2 * NE], -1.0, 1.0, ALU.mult, ALU.add).then_inc(plan, 1)
            dve.wait_ge(plan, 15)
            v.tensor_tensor(at_x[:, :], at_x[:, :], at_i[:, :], ALU.subtract).then_inc(plan, 1)
            dve.wait_ge(plan, 16)
            v.tensor_tensor_reduce(junk[:, 0, :], at_x[:, :], iota_e2[:, :, :].rearrange("p a e -> p (a e)"), 1.0, 0.0,
                                   ALU.mult, ALU.add, sums[:, 0:1]).then_inc(plan, 1)
            v.tensor_tensor_reduce(junk[:, 1, :], at_x[:, :], rowt[:, :], 1.0, 0.0, ALU.mult, ALU.add,
                                   sums[:, 1:2]).then_inc(plan, 1)
            dve.wait_ge(plan, 18)
            v.scalar_tensor_tensor(out=sched[:, 0:1], in0=at_i[:, 2 * NE - 1:2 * NE], scalar=float(NE - 1),
                                   in1=sums[:, 0:1], op0=ALU.mult, op1=ALU.add).then_inc(sched_done, 1)
            v.scalar_tensor_tensor(out=term[:, 0:1], in0=i128[:, :], scalar=used[:, 0:1], in1=sums[:, 1:2],
                                   op0=ALU.mult, op1=ALU.add).then_inc(plan, 1)
            dve.wait_ge(plan, 19)
            v.scalar_tensor_tensor(out=sched[:, 1:2], in0=at_i[:, 2 * NE - 1:2 * NE], scalar=float(NE * CAP),
                                   in1=term[:, 0:1], op0=ALU.mult, op1=ALU.add).then_inc(sched_done, 1)
            v.scalar_tensor_tensor(out=ends[:, 0, :], in0=ebase_b[:, 0, :], scalar=1.0, in1=blk_f[:, :],
                                   op0=ALU.mult, op1=ALU.add).then_inc(plan, 1)
            v.scalar_tensor_tensor(out=ends[:, 1, :], in0=tiles_f[:, :], scalar=float(P // BLK), in1=ebase_b[:, 1, :],
                                   op0=ALU.mult, op1=ALU.add).then_inc(plan, 1)
            v.tensor_tensor(ends[:, 2, :], padr[:, :], eoff_r[:, :], ALU.add).then_inc(plan, 1)
            v.scalar_tensor_tensor(out=ends[:, 3, :], in0=blk_f[:, :], scalar=float(BLK), in1=ebase[:, :],
                                   op0=ALU.mult, op1=ALU.add).then_inc(plan, 1)
            dve.wait_ge(plan, 23)
            for n in range(2):
                v.tensor_tensor(tmp_b[:, n], pick_b[:, :, :], ends[:, n, :].unsqueeze(1).to_broadcast([P, PB, NE]),
                                ALU.mult).then_inc(plan, 1)
            dve.wait_ge(sched_mm, 1)
            v.tensor_copy(sched_i[:, :, :], sched_p.rearrange("p (a n) -> p a n", a=2)).then_inc(sched_out, 1)
            for n in range(2):
                v.tensor_tensor(tmp_r[:, n], pick_r[:, :, :], ends[:, 2 + n, :].unsqueeze(1).to_broadcast([P, PR, NE]),
                                ALU.mult).then_inc(plan, 1)
            dve.wait_ge(plan, 27)
            v.tensor_reduce(pad_b[:, :, :], tmp_b[:, :, :, :], AX.X, ALU.add).then_inc(plan, 1)
            v.tensor_reduce(pad_r[:, :, :], tmp_r[:, :, :, :], AX.X, ALU.add).then_inc(plan, 1)
            dve.wait_ge(plan, 29)
            v.tensor_tensor(pad_b[:, 0, :], pad_b[:, 0, :], off_b[:, :], ALU.add).then_inc(plan, 1)
            v.tensor_tensor(pad_r[:, 0, :], pad_r[:, 0, :], off_r[:, :], ALU.add).then_inc(plan, 1)
            dve.wait_ge(plan, 31)
            v.tensor_tensor(over_b[:, :], pad_b[:, 0, :], pad_b[:, 1, :], ALU.is_ge).then_inc(plan, 1)
            v.tensor_tensor(over_r[:, :], pad_r[:, 0, :], pad_r[:, 1, :], ALU.is_ge).then_inc(plan, 1)
            dve.wait_ge(plan, 33)
            v.scalar_tensor_tensor(out=pad_b_i[:, :], in0=over_b[:, :], scalar=float(NE * CAP), in1=pad_b[:, 0, :],
                                   op0=ALU.mult, op1=ALU.add).then_inc(padr_done, 1)
            v.scalar_tensor_tensor(out=pad_r_i[:, :], in0=over_r[:, :], scalar=float(NE * CAP), in1=pad_r[:, 0, :],
                                   op0=ALU.mult, op1=ALU.add).then_inc(padr_done, 1)

            def hidden(i, g):
                for q in range(2):
                    dve.wait_ge(H_mm, pairs(i, g) + (q + 1))
                    if g >= 2 or not (isinstance(i, int) and i == 0):
                        dve.wait_ge(Y_mm, pairs(i, g) - 2)
                    v.tensor_scalar(hT[:, g % 2, 2 * q:2 * q + 2, :], H_p[q], 0.0, None, ALU.max).then_inc(hid_out, 1)

            def columns(i, g):
                dve.wait_ge(ld_rows[g], dma_count(i) + 16 * GROUP)
                after(dve, y_sent[g], dma_count(i))
                v.tensor_copy(dest[:, g, :], xin[:, g, :, ID].bitcast(I32)).then_inc(cols_out, 1)
                v.tensor_copy(wgt[:, g, :], xin[:, g, :, WEIGHT]).then_inc(cols_out, 1)

            def weighted(i, g):
                after(dve, y_sent[g], dma_count(i))
                dve.wait_ge(cols_out, pairs(i, g) + 2)
                dve.wait_ge(Y_mm, pairs(i, g) + 2)
                for k in range(2, GROUP):
                    v.tensor_scalar(yb[:, g, k, :], Y_p[1][:, k - 2, :], wgt[:, g, k:k + 1], None, ALU.mult).then_inc(y_out_v, 1)

            def dve_group(i, g, first, last):
                hidden(i, g)
                columns(i, g)
                weighted(i, g)

            over_groups(dve, dve_group)

            for c in range(CHUNKS):
                dve.wait_ge(ld_pair[c % DEPTH], 32 * (c // DEPTH + 1))
                t2c = t2[:, c * CG:(c + 1) * CG]
                v.tensor_tensor(t2c, t2c, pair_buf[0][:, c % DEPTH], ALU.add).then_inc(half_sum, 1)
                dve.wait_ge(half_sum, c + 1)
                v.tensor_tensor(t2c, t2c, pair_buf[1][:, c % DEPTH], ALU.add).then_inc(out_sum, 1)

        @block.tensor
        def _(pe):
            m = nc.tensor

            def qk_proj(b, c):
                if b > 0:
                    pe.wait_ge(v_out, v_evacs[0])
                    pe.wait_ge(k_out, 2 * b + c)
                    pe.wait_ge(q_out, 2 * b + c)
                for a in range(CH):
                    for r in range(2):
                        tokens = slice(c * 512 + r * 256, c * 512 + (r + 1) * 256)
                        mm = m.matmul(qk_bank(b, c)[r * 2 * QK:(r + 1) * 2 * QK, 0:256], wqk[:, a, :],
                                      xc[:, b % 2, a, tokens], start=(a == 0), stop=(a == CH - 1))
                        if a == CH - 1:
                            mm.then_inc(qk_mm, 1)
                qk_evacs[0] += 1

            def v_proj(b, j):
                if b == 0:
                    after(pe, v_out, max(0, j + 1 - len(v_banks)))
                elif j < TB - 2:
                    pe.wait_ge(v_out, v_evacs[0])
                    pe.wait_ge(k_out, qk_evacs[0])
                    pe.wait_ge(q_out, qk_evacs[0])
                if b == 0:
                    terms = [(xc[:, 0, a, j * P:(j + 1) * P], wv[:, a, :]) for a in range(CH)]
                else:
                    n = v_no(b - 1, j)
                    pe.wait_ge(wv_lo_done, 1)
                    pe.wait_ge(x_lo_done, n + 1)
                    terms = [(x[:, n % 2, a, :], w[:, a, :]) for a in range(CH)
                             for x, w in ((x_hi, wv_hi), (x_hi, wv_lo), (x_lo, wv_hi))]
                for i, (x, w) in enumerate(terms):
                    mm = m.matmul(v_bank(b, j)[:, 0:C], x, w, start=(i == 0), stop=(i == len(terms) - 1))
                mm.then_inc(v_mm, 1)
                v_evacs[0] += 1

            v_evacs, qk_evacs, bank5_v = [0], [0], [0]
            pe.wait_ge(warm_ready, 1)
            for _ in range(FIRST_WARM):
                m.matmul(bank[7][:, :], warm[:, 0:P], warm[:, :], start=True, stop=True)
            pe.wait_ge(ld_wqk, 32)
            for c in range(2):
                pe.wait_ge(ld_first[c], 16)
                qk_proj(0, c)
            pe.wait_ge(ld_wv, 16)
            for j in range(EARLY_V):
                v_proj(0, j)

            def energies(t):
                b, tb = t // TB, t % TB
                after(pe, centred, t)
                pe.wait_ge(q_out, max(2 * b + 1 + tb // (TB // 2), 2))
                pe.wait_ge(k_out, 2 * (b + 1))
                for w in range(WT):
                    mm = m.matmul(E[:, w * KB * W:(w + 1) * KB * W],
                                  q_s[:, WT * tb + w].rearrange("p g h -> p (g h)"),
                                  k_s[:, b % 2].rearrange("p j v -> p (j v)"), start=True, stop=True)
                mm.then_inc(e_mm, 1)

            energies(0)
            for j in range(EARLY_V, KB):
                v_proj(0, j)
            pe.wait_ge(const_done, 1)
            pe.wait_ge(ld_wmix, 48)

            for s in range(NT + LAST):
                if 0 < s < NT:
                    energies(s)
                work = proj_work(s)
                if work:
                    b, j, chunks = work
                    if 0 < j < TB - 2:
                        v_proj(b, j)
                if s == S_MIX:
                    pe.wait_ge(v_out, KB)
                    for _ in range(FILL_WARM):
                        m.matmul(bank[5][:, :], warm[:, 0:P], warm[:, :], start=True, stop=True)
                t = s - S_POS
                if 0 <= t:
                    pe.wait_ge(hotb_done, t + 1)
                    after(pe, seen_done, t)
                    after(pe, spot_done, t)
                    pe.wait_ge(ex_done, min(t + 2, NT))
                    m.matmul(pos_p, upper[:, :], hotb[:, t % 2], start=True, stop=False)
                    m.matmul(pos_p, ones_b[:, :], seen[:, :], start=False, stop=True).then_inc(pos_mm, 1)
                    if t == NT - 1:
                        m.matmul(cnt_p, ones_b[:, :], hotb[:, t % 2], start=True, stop=False)
                        m.matmul(cnt_p, ones_b[:, :], seen[:, :], start=False, stop=True).then_inc(cnt_mm, 1)
                t = s - S_MIX
                if 0 <= t < NT:
                    pe.wait_ge(u1_done, t + 1)
                    after(pe, uh_out, t)
                    tail = t % TB > 0
                    for a in range(CH):
                        cs = slice(a * P, (a + 1) * P)
                        m.transpose(mix_p[:, a, 0, :], u1[:, t % 3, cs], ident[:, :])
                        mm = m.matmul(mix_p[:, a, 1, :], u1[:, t % 3, cs], band[:, 0:P], start=True, stop=not tail)
                        if tail:
                            mm = m.matmul(mix_p[:, a, 1, 0:REACH], u1[P - REACH:P, (t - 1) % 3, cs],
                                          band[P - REACH:P, P:P + REACH], start=False, stop=True)
                    mm.then_inc(mix_mm, 1)
                if s > NT:
                    for _ in range(DRAIN_WARM):
                        m.matmul(bank[7][:, :], ones_b[:, :], warm[:, :], start=True, stop=True)
                t = s - S_AV
                if 0 <= t < NT:
                    b = t // TB
                    pe.wait_ge(prob_done, t + 1)
                    pe.wait_ge(v_out, (b + 1) * KB)
                    after(pe, t1_done, t)
                    pr = prob[:, t % 2].rearrange("p (j w) v -> p j (w v)", w=WT)
                    for j in range(KB):
                        mm = m.matmul(av_p, pr[:, j, :], vT[:, b % 2, j, :], start=(j == 0), stop=(j == KB - 1))
                    mm.then_inc(av_mm, 1)
                if work:
                    b, j, chunks = work
                    if j == 0:
                        pe.wait_ge(ld_xc[b % 2], xc_loads(b))
                        v_proj(b, j)
                    for c in chunks:
                        qk_proj(b, c)
                t = s - S_NORM2
                if 0 <= t < NT:
                    pe.wait_ge(u2_done, t + 1)
                    after(pe, u2T_out, t)
                    if proj_work(s - 1) and proj_work(s - 1)[2]:
                        pe.wait_ge(v_out, bank5_v[0])
                    for a in range(CH):
                        mm = m.transpose(t2_p[:, a, :], rows[:, t % 4, 0, a * P:(a + 1) * P], ident[:, :])
                    mm.then_inc(u2T_mm, 1)
                t = s - S_MIX
                if 0 <= t < NT:
                    pe.wait_ge(uh_out, t + 1)
                    after(pe, t2_done, t)
                    pe.wait_ge(w_lo_done, 1)
                    splits = [(uh_hi, w12_hi), (uh_hi, w12_lo), (uh_lo, w12_hi)]
                    terms = [(u, w, side, a) for side in range(2) for a in range(CH) for u, w in splits]
                    for i, (u, w, side, a) in enumerate(terms):
                        mm = m.matmul(h_p, u[:, t % 2, a, side, :], w[:, side, a, :],
                                      start=(i == 0), stop=(i == len(terms) - 1))
                    mm.then_inc(h_mm, 1)
                t = s - S_NORM2
                if 0 <= t < NT:
                    pe.wait_ge(u2T_out, t + 1)
                    after(pe, ex_done, t)
                    after(pe, spot_done, t - 1)
                    for a in range(CH):
                        mm = m.matmul(lg_p, u2T[:, t % 2, a, :], sels[:, a, :], start=(a == 0), stop=(a == CH - 1))
                    mm.then_inc(lg_mm, 1)
                if work and work[2]:
                    v_proj(work[0], work[1])
                    bank5_v[0] = v_evacs[0]

            for _ in range(PLAN_WARM):
                m.matmul(bank[7][:, :], ones_b[:, :], warm[:, :], start=True, stop=True)
            pe.wait_ge(sched_done, 2)
            for c in range(2):
                mm = m.matmul(sched_p[:, c * P:(c + 1) * P], sched[:, c:c + 1], ident[:, :], start=True, stop=True)
            mm.then_inc(sched_mm, 1)
            pe.wait_ge(sched_out, 1)
            pe.wait_ge(ld_keys, 32)

            for _ in range(WARM):
                m.matmul(bank[7][:, :], ones_b[:, :], warm[:, :], start=True, stop=True)

            def transpose_pair(i, g, q):
                if q == 0:
                    pe.wait_ge(ld_rows[g], dma_count(i) + 16 * GROUP)
                    after(pe, T_out, pairs(i, g))
                for k in (2 * q, 2 * q + 1):
                    for a in range(CH):
                        mm = m.transpose(T_p[q][:, k % 2, a, :], xin[:, g, k, a * P:(a + 1) * P], ident[:, :])
                mm.then_inc(T_mm, 1)

            def hidden_pair(i, g, q):
                if q == 0:
                    after(pe, hid_out, pairs(i, g))
                pe.wait_ge(T_out, pairs(i, g) + (q + 1))
                for k in (2 * q, 2 * q + 1):
                    for a in range(CH):
                        mm = m.matmul(H_p[q][:, k % 2, :], kk[:, g % 2, k, a, :], uT[:, k, a, :],
                                      start=(a == 0), stop=(a == CH - 1))
                mm.then_inc(H_mm, 1)

            def output_pair(i, g, q, expert):
                after(pe, (y_out_a, y_out_v)[q], pairs(i, g))
                pe.wait_ge(hid_out, pairs(i, g) + (q + 1))
                for k in (2 * q, 2 * q + 1):
                    mm = m.matmul(Y_p[q][:, k % 2, :], hT[:, g % 2, k, :], values_s[:, bass.ds(expert[k], 1), :],
                                  start=True, stop=True)
                mm.then_inc(Y_mm, 1)

            experts = [pe.alloc_register(f"expert{k}") for k in range(GROUP)]

            def pe_group(i, g, first, last):
                expert = loaded(pe, experts, sched_i[0:1, 0, bass.ds(i * (NB * GROUP) + g * GROUP, GROUP)], NE - 1)
                pe.wait_ge(keys_out, groups(i, g) + 1)
                for q in range(2):
                    hidden_pair(i, g, q)
                if not last:
                    for q in range(2):
                        transpose_pair(*following(i, g), q)
                for q in range(2):
                    output_pair(i, g, q, expert)

            for q in range(2):
                transpose_pair(0, 0, q)
            over_groups(pe, pe_group)


def kernel(**inputs):
    import numpy as np
    import concourse.bacc as bacc
    from concourse.bass_utils import run_bass_kernel_spmd

    a = {k: np.asarray(v) for k, v in inputs.items()}
    x = a["x"]
    laid = {
        "x_cm": x.transpose(1, 0, 3, 2).reshape(C, N),
        "x_tok": x.reshape(B, C, HW).transpose(0, 2, 1).reshape(N, C),
        "wqT": a["L0_conv_wq"].T,
        "bq": a["L0_conv_bq"].reshape(QK, 1),
        "wkT": a["L0_conv_wk"].T,
        "bk": a["L0_conv_bk"].reshape(QK, 1),
        "wvT": a["L0_conv_wv"].T,
        "bv": a["L0_conv_bv"].reshape(1, C),
        "gamma": a["L0_conv_gamma"].reshape(1, 1),
        "w1": a["L1_attn_W1"],
        "w2": a["L1_attn_W2"],
        "bias": a["L1_attn_bias"].reshape(1, C),
        "selT": a["L1_ffn_expert_sel"].T,
        "keys": a["L1_ffn_keys"].transpose(1, 0, 2),
        "values": a["L1_ffn_values"].transpose(1, 0, 2),
    }
    laid = {k: np.ascontiguousarray(v) for k, v in laid.items()}

    nc = bacc.Bacc("TRN2", target_bir_lowering=False, num_devices=1)
    args = [nc.dram_tensor(k, v.shape, mybir.dt.from_np(v.dtype), kind="ExternalInput").ap() for k, v in laid.items()]
    args.append(nc.dram_tensor("out", [N, C], F32, kind="ExternalOutput").ap())
    attention_moe(nc, *args)
    r = run_bass_kernel_spmd(nc, [laid], core_ids=[0])
    tokens = r.results[0]["out"]
    return tokens.reshape(B, HW, C).transpose(0, 2, 1).reshape(B, C, H, W)
```
